# Optimizing a Trainium2 kernel written in Bass

```python
import numpy as np
import jax
import jax.numpy as jnp

def _softmax(x, axis=-1):
    return jax.nn.softmax(x, axis=axis)

def _gelu(x):
    return jax.nn.gelu(x, approximate=True)

def _silu(x):
    return jax.nn.silu(x)

def _sigmoid(x):
    return jax.nn.sigmoid(x)

def _layernorm(x, axis=-1, eps=1e-05):
    m = jnp.mean(x, axis=axis, keepdims=True)
    v = jnp.var(x, axis=axis, keepdims=True)
    return (x - m) / jnp.sqrt(v + eps)

def _scatter_add(tgt, idx, src, axis=0):
    return tgt.at[idx].add(src)

def _segment_sum(src, seg, n):
    return jax.ops.segment_sum(src, seg, n)
kernel_name = 'mk_adj_preln_d2_adj_r2_2ebd03'

def setup_inputs(seed: int=0):
    np.random.seed(seed)
    _w = jnp.asarray

    def _rec_inputs():
        import jax
        import jax.numpy as jnp
        _gk = jax.random.key(seed)
        x = -0.0001538 + 1 * jax.random.normal(jax.random.fold_in(_gk, 1), (32, 256, 384), jnp.float32)
        _a = jax.random.bernoulli(jax.random.fold_in(_gk, 2), 0.015625, (32, 256, 256))
        _a = jnp.logical_or(_a, jnp.swapaxes(_a, -1, -2))
        _a = jnp.logical_or(_a, jnp.eye(256, dtype=bool))
        _af = _a.astype(jnp.float32)
        _af = _af * jax.random.uniform(jax.random.fold_in(_gk, 3), (32, 256, 256), jnp.float32, 0.05, 4.42607)
        adj = _af
        return (x, adj)
    x, adj = _rec_inputs()

    def _L0_gnn_setup():
        import jax, jax.numpy as jnp
        import numpy as np
        NUM_HEADS = 12
        HIDDEN = 384
        HEAD = HIDDEN // NUM_HEADS
        B, N = (16, 256)
        key = jax.random.key(seed)
        ks = jax.random.split(key, 9)
        s = 0.02
        return {'x': jax.random.normal(ks[0], (B, N, HIDDEN), jnp.float32), 'spatial_encoding': jax.random.normal(ks[1], (B, N, N), jnp.float32), 'edge_encoding': jax.random.normal(ks[2], (B, N, N), jnp.float32), 'Wq': jax.random.normal(ks[3], (HIDDEN, HIDDEN), jnp.float32) * s, 'Wk': jax.random.normal(ks[4], (HIDDEN, HIDDEN), jnp.float32) * s, 'Wv': jax.random.normal(ks[5], (HIDDEN, HIDDEN), jnp.float32) * s, 'bv': jax.random.normal(ks[6], (HIDDEN,), jnp.float32) * s, 'Wo': jax.random.normal(ks[7], (HIDDEN, HIDDEN), jnp.float32) * s, 'bo': jax.random.normal(ks[8], (HIDDEN,), jnp.float32) * s}
    _L0_gnn_all = _L0_gnn_setup()
    _L0_gnn_in = {k: v for k, v in _L0_gnn_all.items() if k in ('Wq', 'Wk', 'Wv', 'bv', 'Wo', 'bo')}
    del _L0_gnn_all

    def _L1_gnn_setup():
        import jax, jax.numpy as jnp
        import numpy as np
        NUM_HEADS = 12
        HIDDEN = 384
        HEAD = HIDDEN // NUM_HEADS
        SCALE = HIDDEN ** (-0.5)
        key = jax.random.key(seed)
        ks = jax.random.split(key, 8)
        B, N = (16, 256)
        std = HIDDEN ** (-0.5)
        return {'x': jax.random.normal(ks[0], (B, N, HIDDEN), dtype=jnp.float32), 'encoding_bias': jax.random.normal(ks[1], (B, N, N), dtype=jnp.float32), 'Wq': jax.random.normal(ks[2], (HIDDEN, HIDDEN), dtype=jnp.float32) * std, 'Wk': jax.random.normal(ks[3], (HIDDEN, HIDDEN), dtype=jnp.float32) * std, 'Wv': jax.random.normal(ks[4], (HIDDEN, HIDDEN), dtype=jnp.float32) * std, 'bv': jax.random.normal(ks[5], (HIDDEN,), dtype=jnp.float32) * 0.01, 'Wo': jax.random.normal(ks[6], (HIDDEN, HIDDEN), dtype=jnp.float32) * std, 'bo': jax.random.normal(ks[7], (HIDDEN,), dtype=jnp.float32) * 0.01}
    _L1_gnn_all = _L1_gnn_setup()
    _L1_gnn_in = {k: v for k, v in _L1_gnn_all.items() if k in ('Wq', 'Wk', 'Wv', 'bv', 'Wo', 'bo')}
    del _L1_gnn_all
    return {'x': x, 'adj': adj, 'L0_gnn_Wq': _L0_gnn_in['Wq'], 'L0_gnn_Wk': _L0_gnn_in['Wk'], 'L0_gnn_Wv': _L0_gnn_in['Wv'], 'L0_gnn_bv': _L0_gnn_in['bv'], 'L0_gnn_Wo': _L0_gnn_in['Wo'], 'L0_gnn_bo': _L0_gnn_in['bo'], 'L1_gnn_Wq': _L1_gnn_in['Wq'], 'L1_gnn_Wk': _L1_gnn_in['Wk'], 'L1_gnn_Wv': _L1_gnn_in['Wv'], 'L1_gnn_bv': _L1_gnn_in['bv'], 'L1_gnn_Wo': _L1_gnn_in['Wo'], 'L1_gnn_bo': _L1_gnn_in['bo']}

def reference(x, adj, L0_gnn_Wq, L0_gnn_Wk, L0_gnn_Wv, L0_gnn_bv, L0_gnn_Wo, L0_gnn_bo, L1_gnn_Wq, L1_gnn_Wk, L1_gnn_Wv, L1_gnn_bv, L1_gnn_Wo, L1_gnn_bo):
    import jax
    import jax.numpy as jnp

    def _L0_gnn_ref(x, spatial_encoding, edge_encoding, Wq, Wk, Wv, bv, Wo, bo):
        import jax, jax.numpy as jnp
        import numpy as np
        NUM_HEADS = 12
        HIDDEN = 384
        HEAD = HIDDEN // NUM_HEADS
        B, N = (16, 256)
        b, n, h = x.shape
        scale = jnp.asarray(HIDDEN, x.dtype) ** (-0.5)
        q = (x @ Wq.T).reshape(b, n, NUM_HEADS, HEAD)
        k = (x @ Wk.T).reshape(b, n, NUM_HEADS, HEAD)
        v = (x @ Wv.T + bv).reshape(b, n, NUM_HEADS, HEAD)
        bias = (spatial_encoding + edge_encoding)[:, None]
        scores = jnp.einsum('bqhd,bkhd->bhqk', q, k) * scale + bias
        row_nonzero = jnp.any(scores != 0, axis=-1, keepdims=True)
        scores = jnp.where(row_nonzero, scores, -jnp.inf)
        p = jax.nn.softmax(scores, axis=-1)
        p = jnp.nan_to_num(p)
        out = jnp.einsum('bhqk,bkhd->bqhd', p, v).reshape(b, n, h)
        return out @ Wo.T + bo

    def _L1_gnn_ref(x, encoding_bias, Wq, Wk, Wv, bv, Wo, bo):
        import jax, jax.numpy as jnp
        import numpy as np
        NUM_HEADS = 12
        HIDDEN = 384
        HEAD = HIDDEN // NUM_HEADS
        SCALE = HIDDEN ** (-0.5)
        B, N, _ = x.shape
        q = (x @ Wq.T).reshape(B, N, NUM_HEADS, HEAD)
        k = (x @ Wk.T).reshape(B, N, NUM_HEADS, HEAD)
        v = (x @ Wv.T + bv).reshape(B, N, NUM_HEADS, HEAD)
        a = jnp.einsum('bnhd,bmhd->bhnm', q, k) * SCALE + encoding_bias[:, None, :, :]
        pad_mask = jnp.all(a == 0, axis=-1)
        a = jnp.where(pad_mask[..., None], -jnp.inf, a)
        a = jax.nn.softmax(a, axis=-1)
        a = jnp.nan_to_num(a)
        o = jnp.einsum('bhnm,bmhd->bnhd', a, v).reshape(B, N, HIDDEN)
        return o @ Wo.T + bo
    h = jnp.maximum(_layernorm(x, axis=-1), 0.0)
    x = x + _L0_gnn_ref(h, adj, adj, L0_gnn_Wq, L0_gnn_Wk, L0_gnn_Wv, L0_gnn_bv, L0_gnn_Wo, L0_gnn_bo)
    h = jnp.maximum(_layernorm(x, axis=-1), 0.0)
    x = x + _L1_gnn_ref(h, adj, L1_gnn_Wq, L1_gnn_Wk, L1_gnn_Wv, L1_gnn_bv, L1_gnn_Wo, L1_gnn_bo)
    return x

_drawn_inputs = setup_inputs


def setup_inputs(seed=0):
    import zlib

    import numpy as np

    out = dict(_drawn_inputs(seed))
    spreads = {}
    factors = {'L0_gnn_Wq': 8.0,
     'L0_gnn_Wk': 8.0,
     'L0_gnn_bv': 6.3,
     'L0_gnn_bo': 2.833,
     'L1_gnn_Wq': 4.966,
     'L1_gnn_Wk': 4.941,
     'L1_gnn_bv': 5.607,
     'L1_gnn_bo': 6.188}
    for name, (base, spread) in spreads.items():
        noise = np.random.default_rng([zlib.crc32(name.encode()), seed]).standard_normal(out[name].shape)
        drawn = base * np.exp(spread * noise) if base else spread * noise
        out[name] = jnp.asarray(drawn.astype(out[name].dtype))
    for name, factor in factors.items():
        out[name] = (out[name] * factor).astype(out[name].dtype)
    return out
```

```python
from contextlib import ExitStack

import concourse.bass as bass
from concourse import mybir

F32 = mybir.dt.float32
F32R = mybir.dt.float32r
ALU = mybir.AluOpType
ACT = mybir.ActivationFunctionType
AX = mybir.AxisListType

P = 128
EPS = 1e-5
LARGEST = 3.4028234663852886e38
GROUP = 4
COPIES = 3

TRANSPOSE_ROWS_STEP = 0
QK_STEPS = ((1, 2), (3, 4), (5, 6))
SHARES_STEPS = {0: 7, 1: 11, 2: 3}
OUT_STEPS = (7, 8)
V_STEPS = (9, 10)
VALUES_STEPS = {0: 6, 1: 10, 2: 2}
ROWS_BANK, QK_BANK, SHARES_BANK, OUT_BANK, V_BANK = (0, 1), (0, 0, 1), (0, 1, 1), (1, 0), (1, 0)


def is_act_copy(step):
    return step not in (1, 3, 6, 8, 11)


ACT_COPIES = sum(is_act_copy(s) for s in range(12))
DVE_COPIES = 12 - ACT_COPIES


class Unit:

    def __init__(self, k, turn=None, units=64):
        self.k, self.turn, self.units = k, turn, units
        first, last = k == 0, turn is None and k == units - 1
        self.layer = 0 if (k % 2 or first) and not last else 1
        self.t = 0 if first else units // 2 - 1 if last else (k + 1) // 2 if k % 2 else (k - 2) // 2

    def graph(self):
        return self.t if self.turn is None else self.turn * 2 + self.t

    def count(self, per_unit, done):
        c = self.k * per_unit + done
        return max(c, 0) if self.turn is None else self.turn * (4 * per_unit) + c

    def before(self, n):
        return Unit(self.k - n, self.turn, self.units)


def build(nc, x, adj, weights, biases, out):
    B, N, H = x.shape
    HEAD = 32
    HEADS = H // HEAD
    GROUPS = HEADS // GROUP
    CH = H // P
    TILES = N // P
    UNITS = 2 * B
    QUADS = P // HEAD
    ROW = CH * N
    SCALE = float(H) ** -0.5

    with ExitStack() as ctx:
        def sb(name, shape, dt=F32):
            return ctx.enter_context(nc.sbuf_tensor(name, shape, dt))

        def psum(name):
            return ctx.enter_context(nc.psum_tensor(name, [P, 512], F32))

        def sem(name):
            return ctx.enter_context(nc.semaphore(name))

        w_high = {(l, n): sb(f"w_high_{l}{n}", [P, CH, H], F32R) for l in range(2) for n in "qkvo"}
        w_low = {(l, n): sb(f"w_low_{l}{n}", [P, CH, H], F32R) for l in range(2) for n in "qkvo"}
        v_bias = [sb(f"v_bias{l}", [P, H]) for l in range(2)]
        o_bias = [sb(f"o_bias{l}", [P, H]) for l in range(2)]
        identity = sb("identity", [P, P])
        minus_half = sb("minus_half", [P, TILES])

        rows = [[sb(f"rows{l}{i}", [P, TILES, H]) for i in range(2)] for l in range(2)]
        bias = [sb(f"bias{i}", [P, TILES, N]) for i in range(4)]
        stats = sb("stats", [P, TILES, 6])
        mean_var = sb("mean_var", [P, TILES, 2])
        var_eps = sb("var_eps", [P, TILES])
        inv_dev = sb("inv_dev", [P, TILES])
        normed = sb("normed", [P, TILES, H])
        rowsT_high = sb("rowsT_high", [P, CH, N], F32R)
        rowsT_low = sb("rowsT_low", [P, CH, N], F32R)
        split_qk = sb("split_qk", [P, 4, ROW], F32R)
        stack = sb("stack", [COPIES * HEAD, QUADS, 2, ROW], F32R)
        values = [sb(f"values{i}", [P, TILES, H]) for i in range(2)]
        NEG, PROB, PROBT = 4, 4, 6
        neg = sb("neg", [P, NEG, TILES, N])
        prob = sb("prob", [P, PROB, TILES, N])
        probT = sb("probT", [P, PROBT, TILES, N])
        neg_max = [sb(f"neg_max{i}", [P, HEADS, TILES]) for i in range(2)]
        sums = [sb(f"sums{i}", [P, HEADS, TILES]) for i in range(2)]
        half = sb("half", [P, GROUP, TILES, N // 2])
        quarter = sb("quarter", [P, GROUP, TILES, N // 4])
        eighth = sb("eighth", [P, GROUP, TILES, N // 8])
        total = sb("total", [P, TILES, GROUP])
        nonzero = sb("nonzero", [P, TILES, GROUP])
        inverse = sb("inverse", [P, TILES, GROUP])
        shares = sb("shares", [P, 2, TILES * GROUP, HEAD])
        sharesT = sb("sharesT", [P, N])
        headsT = sb("headsT", [P, 2, N])
        headsT_high = sb("headsT_high", [P, GROUPS, N], F32R)
        headsT_low = sb("headsT_low", [P, GROUPS, N], F32R)

        score_bank = [psum(f"score_bank{i}") for i in range(2)]
        probT_bank = [psum(f"probT_bank{i}") for i in range(2)]
        values_bank = [psum(f"values_bank{i}") for i in range(2)]
        misc_bank = [psum(f"misc_bank{i}") for i in range(2)]

        staging = [neg[:, :, :, :].rearrange("p a b c -> p (a b c)")[:, 0:CH * H],
                   prob[:, :, :, :].rearrange("p a b c -> p (a b c)")[:, 0:CH * H],
                   probT[:, :, :, :].rearrange("p a b c -> p (a b c)")[:, 0:CH * H],
                   probT[:, :, :, :].rearrange("p a b c -> p (a b c)")[:, 3 * 512:3 * 512 + CH * H]]
        matrices = [(l, n) for l in range(2) for n in "qkvo"]

        passed = sem("passed")
        w_loaded = [sem(f"w_loaded{i}") for i in range(4)]
        bias_rows_loaded = sem("bias_rows_loaded")
        rows_loaded = [sem(f"rows_loaded{i}") for i in range(2)]
        bias_loaded = [sem(f"bias_loaded{i}") for i in range(4)]
        stacked = [sem(f"stacked{g}") for g in range(QUADS)]
        stored = [sem(f"stored{i}") for i in range(2)]
        w_high_done = sem("w_high_done")
        exp_done = sem("exp_done")
        rows_high_done = sem("rows_high_done")
        qk_high_done = sem("qk_high_done")
        sharesT_done = sem("sharesT_done")
        act_copy_done = sem("act_copy_done")
        w_low_done = sem("w_low_done")
        neg_done = sem("neg_done")
        rows_low_done = sem("rows_low_done")
        qk_low_done = sem("qk_low_done")
        values_done = sem("values_done")
        stats_done = sem("stats_done")
        mean_done = sem("mean_done")
        normed_done = sem("normed_done")
        heads_done = sem("heads_done")
        result_done = sem("result_done")
        guard_done = sem("guard_done")
        shares_done = sem("shares_done")
        dve_copy_done = sem("dve_copy_done")
        scores_done = sem("scores_done")
        probT_ready = sem("probT_ready")
        heads_ready = sem("heads_ready")
        rowsT_ready = sem("rowsT_ready")
        qk_ready = sem("qk_ready")
        v_ready = sem("v_ready")
        sharesT_ready = sem("sharesT_ready")
        out_ready = sem("out_ready")
        constants_done = sem("constants_done")
        half_done = sem("half_done")
        quarter_done = sem("quarter_done")
        eighth_done = sem("eighth_done")
        eps_done = sem("eps_done")
        inv_dev_done = sem("inv_dev_done")
        heads_high_done = sem("heads_high_done")
        heads_split_done = sem("heads_split_done")
        residual_done = sem("residual_done")

        def program(slot, loop):
            def u(k, turn=None):
                return Unit(k, turn, UNITS)
            slot(None, u(0), None, u(1))
            slot(u(0), u(1), None, None)
            slot(u(1), None, u(0), u(2))
            slot(None, u(2), u(1), u(3))
            slot(u(2), u(3), None, u(4))
            turns = (UNITS - 6) // 4
            with loop(0, turns) as turn:
                for k in range(3, 7):
                    slot(u(k, turn), u(k + 1, turn), u(k - 1, turn), u(k + 2, turn))
            for k in range(3 + 4 * turns, UNITS - 3):
                slot(u(k), u(k + 1), u(k - 1), u(k + 2))
            k = UNITS - 1
            slot(u(k - 2), u(k - 1), u(k - 3), None)
            slot(u(k - 1), None, u(k - 2), u(k))
            slot(None, u(k), u(k - 1), None)
            slot(u(k), None, None, None)
            slot(None, None, u(k), None)

        def last_group(attend, output, kept):
            return attend.before(1) if attend is not None and attend.k > 0 else kept

        block = ctx.enter_context(nc.Block())

        def rows_of(u):
            return rows[u.layer][u.t % 2]

        @block.sync
        def _(sync):
            def load_weights(i):
                l, n = matrices[i]
                sync.dma_start(staging[i % 4].rearrange("p (c o) -> p c o", c=CH),
                               weights[l, n].rearrange("(c p) o -> p c o", p=P)).then_inc(w_loaded[i % 4], 16)

            def load_unit(u):
                sync.wait_ge(neg_done, u.before(4).count(2 * HEADS, 2 * HEADS))
                sync.dma_start(bias[u.k % 4][:, :, :],
                               adj[bass.ds(u.graph(), 1)].rearrange("a (i p) k -> p (a i) k", p=P)
                               ).then_inc(bias_loaded[u.k % 4], 16)
                if u.layer == 0:
                    sync.wait_ge(result_done, u.before(4 if u.k != 3 else 3).count(TILES, TILES))
                    sync.dma_start(rows_of(u)[:, :, :],
                                   x[bass.ds(u.graph(), 1)].rearrange("a (i p) c -> p (a i) c", p=P)
                                   ).then_inc(rows_loaded[u.t % 2], 16)

            def stack_quadrant(u, g):
                sync.wait_ge(scores_done, u.before(1).count(HEADS, CH * (g + 1)))
                quad = split_qk[g * HEAD:(g + 1) * HEAD, :, :].bitcast(F32)
                for part, (q, k) in enumerate(((1, 2), (1, 3), (0, 2))):
                    sync.dma_start(stack[part * HEAD:(part + 1) * HEAD, g, :, :].bitcast(F32),
                                   quad[:, q:k + 1:k - q, :]).then_inc(stacked[g], 16)

            load_weights(0)
            load_unit(Unit(0))
            load_weights(1)
            load_weights(2)
            load_weights(3)
            for l in range(2):
                for tile, name in ((v_bias, "v"), (o_bias, "o")):
                    sync.dma_start(tile[l][:, :], biases[l, name].rearrange("(a c) -> a c", a=1).to_broadcast([P, H])
                                   ).then_inc(bias_rows_loaded, 16)
            load_unit(Unit(1))
            for i in range(4, 8):
                sync.wait_ge(w_low_done, i - 3)
                load_weights(i)

            def slot(attend, project, output, norm):
                if norm is not None and norm.k > 1:
                    load_unit(norm)
                if project is not None:
                    sync.wait_ge(qk_low_done, project.count(CH, CH))
                    sync.sem_inc(passed, 1)
                    for g in range(QUADS - 1):
                        stack_quadrant(project, g)
                if output is not None and output.layer == 1:
                    sync.wait_ge(result_done, output.count(TILES, TILES))
                    sync.dma_start(out[bass.ds(output.graph(), 1)].rearrange("a (i p) c -> p (a i) c", p=P),
                                   rows_of(output)[:, :, :]).then_inc(stored[output.t % 2], 16)
                if project is not None:
                    stack_quadrant(project, QUADS - 1)

            program(slot, sync.Fori)
            for i in range(2):
                sync.wait_ge(stored[i], 16 * (B // 2))

        @block.gpsimd
        def _(pool):
            nc.gpsimd.memset(identity[:, :], 0.0).then_inc(constants_done, 1)
            nc.gpsimd.memset(minus_half[:, :], -0.5).then_inc(constants_done, 1)
            pool.wait_ge(constants_done, 2)
            nc.gpsimd.affine_select(out=identity[:, :], in_=identity[:, :], compare_op=ALU.not_equal, fill=1.0,
                                    base=0, pattern=[[-1, P]], channel_multiplier=1).then_inc(constants_done, 1)

            def invert_deviation(u):
                pool.wait_ge(mean_done, u.count(TILES, TILES))
                pool.sem_inc(passed, 1)
                nc.gpsimd.tensor_scalar(var_eps[:, :], mean_var[:, :, 1], EPS, None, ALU.add).then_inc(eps_done, 1)
                pool.wait_ge(eps_done, u.count(1, 1))
                nc.gpsimd.tensor_tensor(inv_dev[:, :], var_eps[:, :], minus_half[:, :], ALU.pow
                                        ).then_inc(inv_dev_done, 1)

            def add_half(u, step):
                pool.wait_ge(neg_done, u.count(2 * HEADS, 2 * step + 2))
                n = neg[:, step % NEG, :, :]
                nc.gpsimd.tensor_tensor(half[:, step % GROUP, :, :], n[:, :, 0:N // 2], n[:, :, N // 2:N], ALU.add
                                        ).then_inc(half_done, 1)

            def add_rest(u, g):
                pool.wait_ge(half_done, u.count(HEADS, GROUP * (g + 1)))
                nc.gpsimd.tensor_tensor(quarter[:, :, :, :], half[:, :, :, 0:N // 4], half[:, :, :, N // 4:N // 2],
                                        ALU.add).then_inc(quarter_done, 1)
                pool.wait_ge(quarter_done, u.count(GROUPS, g + 1))
                pool.wait_ge(guard_done, u.count(3 * GROUPS, 3 * g))
                nc.gpsimd.tensor_tensor(eighth[:, :, :, :], quarter[:, :, :, 0:N // 8], quarter[:, :, :, N // 8:N // 4],
                                        ALU.add).then_inc(eighth_done, 1)

            def split_heads(u, g):
                i = (u.k * GROUPS + g) % 2
                if g == 0:
                    pool.wait_ge(out_ready, u.before(1).count(TILES, TILES))
                pool.wait_ge(heads_done, u.count(GROUPS, g + 1))
                pool.sem_inc(passed, 1)
                nc.gpsimd.tensor_scalar(headsT_high[:, g, :], headsT[:, i, :], 1.0, 0.0, ALU.mult, ALU.add
                                        ).then_inc(heads_high_done, 1)
                pool.wait_ge(heads_high_done, u.count(GROUPS, g + 1))
                nc.gpsimd.tensor_tensor(headsT_low[:, g, :], headsT[:, i, :], headsT_high[:, g, :].bitcast(F32),
                                        ALU.subtract).then_inc(heads_split_done, 1)

            def add_output_bias(u):
                if u.k == 0:
                    pool.wait_ge(bias_rows_loaded, 16 * 4)
                pool.wait_ge(normed_done, u.count(TILES, TILES))
                r = rows_of(u)
                for i in range(TILES):
                    add = nc.gpsimd.tensor_tensor(r[:, i, :], r[:, i, :], o_bias[u.layer][:, :], ALU.add)
                add.then_inc(residual_done, 1)

            invert_deviation(Unit(0))
            kept = [None]

            def slot(attend, project, output, norm):
                kept[0] = last = last_group(attend, output, kept[0])
                for step in range(HEADS):
                    if attend is not None:
                        add_half(attend, step)
                        if step % GROUP == GROUP - 1:
                            add_rest(attend, step // GROUP)
                    if step == 1 and project is not None:
                        add_output_bias(project)
                    if output is not None and step == 0:
                        split_heads(output, 1)
                    if output is not None and step == 4:
                        split_heads(output, 2)
                    if attend is not None and step == 8:
                        split_heads(attend, 0)
                    if step == 10 and norm is not None:
                        invert_deviation(norm)

            program(slot, pool.Fori)

        @block.scalar
        def _(act):
            for i, (l, n) in enumerate(matrices):
                act.wait_ge(w_loaded[i % 4], 16 * (i // 4 + 1))
                scale = (SCALE / 2 if l == 0 else SCALE) if n == "q" else 1.0
                nc.scalar.activation(w_high[l, n][:, :, :].rearrange("p c o -> p (c o)"), staging[i % 4], ACT.Copy,
                                     scale=scale).then_inc(w_high_done, 1)

            def exps(u, step):
                act.wait_ge(probT_ready, u.count(HEADS, step + 1 - PROB))
                for q in range(TILES):
                    act.wait_ge(neg_done, u.count(2 * HEADS, 2 * step + q + 1))
                    nc.scalar.activation(prob[:, step % PROB, q, :], neg[:, step % NEG, q, :], ACT.Exp, scale=-1.0,
                                         bias=neg_max[u.k % 2][:, step, q:q + 1],
                                         accum_out=sums[u.k % 2][:, step, q:q + 1]).then_inc(exp_done, 1)

            def copy_probT(u, step):
                n = sum(is_act_copy(s) for s in range(step))
                act.wait_ge(probT_ready, u.count(HEADS, step + 1))
                act.wait_ge(heads_ready, u.count(GROUPS, (step - PROBT) // GROUP + 1))
                nc.scalar.activation(probT[:, step % PROBT, :, :].rearrange("p a b -> p (a b)"),
                                     probT_bank[step % 2][:, :], ACT.Copy).then_inc(act_copy_done, 1)

            def rows_high(u, i):
                act.wait_ge(rowsT_ready, u.count(TILES, i + 1))
                act.wait_ge(v_ready, u.count(TILES, 0))
                nc.scalar.activation(rowsT_high[:, :, i * P:(i + 1) * P],
                                     misc_bank[ROWS_BANK[i]][:, 0:H].rearrange("p (c t) -> p c t", c=CH), ACT.Relu
                                     ).then_inc(rows_high_done, 1)

            def qk_high(u, c):
                act.wait_ge(qk_ready, u.count(CH, c + 1))
                if c == 0:
                    for g in range(QUADS):
                        act.wait_ge(stacked[g], u.count(16 * COPIES, 0))
                nc.scalar.activation(split_qk[:, 1:3, c * N:(c + 1) * N],
                                     misc_bank[QK_BANK[c]][:, :].rearrange("p (a n) -> p a n", a=2), ACT.Copy
                                     ).then_inc(qk_high_done, 1)

            def copy_sharesT(u, g):
                act.wait_ge(sharesT_ready, u.count(GROUPS, g + 1))
                act.wait_ge(heads_done, u.count(GROUPS, g))
                nc.scalar.activation(sharesT[:, :], misc_bank[SHARES_BANK[g]][:, 0:N], ACT.Copy
                                     ).then_inc(sharesT_done, 1)

            def slot(attend, project, output, norm):
                for step in range(HEADS):
                    if attend is not None:
                        exps(attend, step)
                        if step >= 1 and is_act_copy(step - 1):
                            copy_probT(attend, step - 1)
                    if step == 0 and output is not None and is_act_copy(HEADS - 1):
                        copy_probT(output, HEADS - 1)
                    if step == TRANSPOSE_ROWS_STEP and project is not None:
                        for i in range(TILES):
                            rows_high(project, i)
                    for c in range(CH):
                        if step == QK_STEPS[c][1] and project is not None:
                            qk_high(project, c)
                    if step == SHARES_STEPS[2] and output is not None:
                        copy_sharesT(output, 2)
                    for g in range(2):
                        if step == SHARES_STEPS[g] and attend is not None:
                            copy_sharesT(attend, g)

            program(slot, act.Fori)

        @block.vector
        def _(dve):
            def statistics(u, i):
                if u.layer == 0:
                    dve.wait_ge(rows_loaded[u.t % 2], rows_count(u))
                else:
                    dve.wait_ge(result_done, before_layer(u).count(TILES, i + 1))
                nc.vector.bn_stats(stats[:, i, :], rows_of(u)[:, i, :]).then_inc(stats_done, 1)

            def rows_count(u):
                return 16 * (u.t // 2 + 1) if u.turn is None else u.turn * 16 + 16 * (u.t // 2 + 1)

            def bias_count(u):
                return 16 * (u.k // 4 + 1) if u.turn is None else u.turn * 16 + 16 * (u.k // 4 + 1)

            def before_layer(u):
                k = max(2 * u.t - 1, 0)
                return Unit(k, u.turn, UNITS)

            def mean(u, i):
                dve.wait_ge(stats_done, u.count(TILES, i + 1))
                dve.wait_ge(eps_done, u.count(1, 0))
                dve.sem_inc(passed, 1)
                nc.vector.bn_aggr(mean_var[:, i, :], stats[:, i, :]).then_inc(mean_done, 1)

            def normalise(u, i):
                dve.wait_ge(inv_dev_done, u.count(1, 1))
                dve.wait_ge(rowsT_ready, u.count(TILES, 0))
                nc.vector.tensor_scalar(normed[:, i, :], rows_of(u)[:, i, :], mean_var[:, i, 0:1], inv_dev[:, i:i + 1],
                                        ALU.subtract, ALU.mult).then_inc(normed_done, 1)

            def norm_all(u):
                for i in range(TILES):
                    statistics(u, i)
                for i in range(TILES):
                    mean(u, i)

            def rows_low(u, i):
                dve.wait_ge(rows_high_done, u.count(TILES, i + 1))
                where = slice(i * P, (i + 1) * P)
                nc.vector.scalar_tensor_tensor(
                    out=rowsT_low[:, :, where], in0=misc_bank[ROWS_BANK[i]][:, 0:H].rearrange("p (c t) -> p c t", c=CH),
                    scalar=0.0, in1=rowsT_high[:, :, where].bitcast(F32), op0=ALU.max, op1=ALU.subtract
                ).then_inc(rows_low_done, 1)

            def qk_low(u, c):
                dve.wait_ge(qk_high_done, u.count(CH, c + 1))
                where = slice(c * N, (c + 1) * N)
                nc.vector.tensor_tensor(split_qk[:, 0:4:3, where],
                                        misc_bank[QK_BANK[c]][:, :].rearrange("p (a n) -> p a n", a=2),
                                        split_qk[:, 1:3, where].bitcast(F32), ALU.subtract).then_inc(qk_low_done, 1)

            def add_value_bias(u, i):
                dve.wait_ge(v_ready, u.count(TILES, i + 1))
                dve.wait_ge(heads_ready, u.before(1).count(GROUPS, 0))
                nc.vector.tensor_tensor(values[u.k % 2][:, i, :], misc_bank[V_BANK[i]][:, 0:H], v_bias[u.layer][:, :],
                                        ALU.add).then_inc(values_done, 1)

            def negate_scores(u, step):
                if step == 0:
                    dve.wait_ge(bias_loaded[u.k % 4], bias_count(u))
                dve.wait_ge(scores_done, u.count(HEADS, step + 1))
                dve.wait_ge(exp_done, u.count(2 * HEADS, 2 * (step + 1 - NEG)))
                dve.wait_ge(half_done, u.count(HEADS, step + 1 - NEG))
                dve.sem_inc(passed, 1)
                for q in range(TILES):
                    nc.vector.tensor_tensor_reduce(
                        out=neg[:, step % NEG, q, :], in0=score_bank[step % 2][:, q * N:(q + 1) * N],
                        in1=bias[u.k % 4][:, q, :], scale=-2.0 if u.layer == 0 else -1.0, scalar=LARGEST,
                        op0=ALU.add, op1=ALU.min, accum_out=neg_max[u.k % 2][:, step, q:q + 1]
                    ).then_inc(neg_done, 1)

            def copy_probT(u, step):
                dve.wait_ge(probT_ready, u.count(HEADS, step + 1))
                dve.wait_ge(heads_ready, u.count(GROUPS, (step - PROBT) // GROUP + 1))
                nc.vector.tensor_copy(probT[:, step % PROBT, :, :].rearrange("p a b -> p (a b)"),
                                      probT_bank[step % 2][:, :]).then_inc(dve_copy_done, 1)

            def share(u, g):
                heads = slice(GROUP * g, GROUP * (g + 1))
                dve.wait_ge(exp_done, u.count(2 * HEADS, 2 * GROUP * (g + 1)))
                nc.vector.reciprocal(inverse[:, :, :], sums[u.k % 2][:, heads, :].rearrange("p h q -> p q h")).then_inc(guard_done, 1)
                dve.wait_ge(eighth_done, u.count(GROUPS, g + 1))
                nc.vector.tensor_reduce(total[:, :, :].rearrange("p q h -> p h q"), eighth[:, :, :, :], AX.X, ALU.add).then_inc(guard_done, 1)
                dve.wait_ge(guard_done, u.count(3 * GROUPS, 3 * g + 2))
                nc.vector.scalar_tensor_tensor(out=nonzero[:, :, :], in0=total[:, :, :], scalar=-1.0,
                                               in1=neg_max[u.k % 2][:, heads, :].rearrange("p h q -> p q h"), op0=ALU.mult, op1=ALU.min
                                               ).then_inc(guard_done, 1)
                dve.wait_ge(guard_done, u.count(3 * GROUPS, 3 * g + 3))
                wide = [t[:, :, :].rearrange("p q (h a) -> p (q h) a", a=1).to_broadcast([P, TILES * GROUP, HEAD])
                        for t in (nonzero, inverse)]
                nc.vector.scalar_tensor_tensor(out=shares[:, (u.k * GROUPS + g) % 2, :, :], in0=wide[0],
                                               scalar=0.0, in1=wide[1], op0=ALU.not_equal, op1=ALU.mult
                                               ).then_inc(shares_done, 1)

            def scale_heads(u, g):
                i = (u.k * GROUPS + g) % 2
                dve.wait_ge(heads_ready, u.count(GROUPS, g + 1))
                dve.wait_ge(sharesT_done, u.count(GROUPS, g + 1))
                dve.wait_ge(heads_split_done, u.count(GROUPS, g - 1))
                nc.vector.tensor_tensor(headsT[:, i, :], values_bank[i][:, 0:N], sharesT[:, :], ALU.mult
                                        ).then_inc(heads_done, 1)

            def result(u, i):
                dve.wait_ge(out_ready, u.count(TILES, i + 1))
                dve.wait_ge(residual_done, u.count(1, 1))
                to = rows[1][u.t % 2]
                if u.layer == 0 and i == 0:
                    dve.wait_ge(stored[u.t % 2], stored_count(u))
                nc.vector.tensor_tensor(to[:, i, :], misc_bank[OUT_BANK[i]][:, 0:H], rows_of(u)[:, i, :], ALU.add
                                        ).then_inc(result_done, 1)

            def stored_count(u):
                return 16 * (u.t // 2) if u.turn is None else u.turn * 16 + 16 * (u.t // 2)

            def split_low(i):
                l, n = matrices[i]
                dve.wait_ge(w_high_done, i + 1)
                scale = (SCALE / 2 if l == 0 else SCALE) if n == "q" else 1.0
                nc.vector.scalar_tensor_tensor(
                    out=w_low[l, n][:, :, :].rearrange("p c o -> p (c o)"), in0=staging[i % 4], scalar=scale,
                    in1=w_high[l, n][:, :, :].rearrange("p c o -> p (c o)").bitcast(F32), op0=ALU.mult, op1=ALU.subtract
                ).then_inc(w_low_done, 1)

            norm_all(Unit(0))
            for i in range(3):
                split_low(i)
            for i in range(TILES):
                normalise(Unit(0), i)
            for i in range(3, 8):
                split_low(i)
            dve.wait_ge(bias_rows_loaded, 16 * 4)

            def slot(attend, project, output, norm):
                for step in range(HEADS):
                    if attend is not None:
                        negate_scores(attend, step)
                        if step >= 2 and not is_act_copy(step - 2):
                            copy_probT(attend, step - 2)
                    if output is not None and step < 2 and not is_act_copy(HEADS + step - 2):
                        copy_probT(output, HEADS + step - 2)
                    if step == TRANSPOSE_ROWS_STEP + 1 and project is not None:
                        for i in range(TILES):
                            rows_low(project, i)
                    for c in range(CH):
                        if step == QK_STEPS[c][1] + 1 and project is not None:
                            qk_low(project, c)
                    if output is not None:
                        if step == 0:
                            scale_heads(output, 1)
                        if step == 2:
                            share(output, 2)
                        if step == 4:
                            scale_heads(output, 2)
                        for i in range(TILES):
                            if step == OUT_STEPS[i] + 1:
                                result(output, i)
                    if attend is not None:
                        if step == 6:
                            share(attend, 0)
                        if step == 8:
                            scale_heads(attend, 0)
                        if step == 10:
                            share(attend, 1)
                    if project is not None:
                        for i in range(TILES):
                            if step == V_STEPS[i] + 1:
                                add_value_bias(project, i)
                    if norm is not None:
                        if step == 9:
                            statistics(norm, 0)
                        if step == 10:
                            statistics(norm, 1)
                            mean(norm, 0)
                            mean(norm, 1)
                        if step == 11:
                            normalise(norm, 0)
                            normalise(norm, 1)

            program(slot, dve.Fori)

        @block.tensor
        def _(pe):
            def copied(u, steps):
                n = sum(is_act_copy(s) for s in range(steps))
                return n, steps - n

            def scores(u, step):
                g, c = step // CH, step % CH
                if c == 0:
                    pe.wait_ge(stacked[g], u.count(16 * COPIES, 16 * COPIES))
                pe.wait_ge(neg_done, u.count(2 * HEADS, 2 * (step - 1)))
                for q in range(TILES):
                    mm = nc.tensor.matmul(score_bank[step % 2][:, q * N:(q + 1) * N],
                                          stack[:, g, 0, c * N + q * P:c * N + (q + 1) * P],
                                          stack[:, g, 1, c * N:(c + 1) * N], start=True, stop=True)
                mm.then_inc(scores_done, 1)

            def transposes(u, step):
                pe.wait_ge(exp_done, u.count(2 * HEADS, 2 * (step + 1)))
                if step >= 2:
                    n = sum(is_act_copy(s) for s in range(step - 1))
                    pe.wait_ge(act_copy_done, u.count(ACT_COPIES, n))
                    pe.wait_ge(dve_copy_done, u.count(DVE_COPIES, step - 1 - n))
                else:
                    n = sum(is_act_copy(s) for s in range(HEADS + step - 1))
                    pe.wait_ge(act_copy_done, u.before(1).count(ACT_COPIES, n))
                    pe.wait_ge(dve_copy_done, u.before(1).count(DVE_COPIES, HEADS + step - 1 - n))
                for k in range(TILES):
                    for q in range(TILES):
                        mm = nc.tensor.transpose(probT_bank[step % 2][:, k * N + q * P:k * N + (q + 1) * P],
                                                 prob[:, step % PROB, q, k * P:(k + 1) * P], identity[:, :])
                mm.then_inc(probT_ready, 1)

            def weigh_values(u, g):
                i = (u.k * GROUPS + g) % 2
                n = sum(is_act_copy(s) for s in range(GROUP * (g + 1)))
                pe.wait_ge(act_copy_done, u.count(ACT_COPIES, n))
                pe.wait_ge(dve_copy_done, u.count(DVE_COPIES, GROUP * (g + 1) - n))
                if g == 0:
                    pe.wait_ge(values_done, u.count(TILES, TILES))
                pe.wait_ge(heads_done, u.count(GROUPS, g - 1))
                for k in range(TILES):
                    for a in range(GROUP):
                        h = GROUP * g + a
                        mm = nc.tensor.matmul(values_bank[i][a * HEAD:(a + 1) * HEAD, 0:N],
                                              values[u.k % 2][:, k, h * HEAD:(h + 1) * HEAD],
                                              probT[:, h % PROBT, k, :], start=(k == 0), stop=(k == TILES - 1))
                mm.then_inc(heads_ready, 1)

            def transpose_rows(u, i):
                pe.wait_ge(normed_done, u.count(TILES, i + 1))
                for c in range(CH):
                    mm = nc.tensor.transpose(misc_bank[ROWS_BANK[i]][:, c * P:(c + 1) * P],
                                             normed[:, i, c * P:(c + 1) * P], identity[:, :])
                mm.then_inc(rowsT_ready, 1)

            def project_qk(u, c, which):
                if which == 0 and c == 0:
                    pe.wait_ge(rows_low_done, u.count(TILES, TILES))
                    if u.k < 2:
                        pe.wait_ge(w_low_done, 2)
                high, low = w_high[u.layer, "qk"[which]], w_low[u.layer, "qk"[which]]
                cols = slice(c * P, (c + 1) * P)
                into = misc_bank[QK_BANK[c]][:, which * N:(which + 1) * N]
                for k in range(CH):
                    for n, (w, r) in enumerate(((low, rowsT_high), (high, rowsT_low), (high, rowsT_high))):
                        mm = nc.tensor.matmul(into, w[:, k, cols], r[:, k, :], start=(k == 0 and n == 0),
                                              stop=(k == CH - 1 and n == 2))
                if which == 1:
                    mm.then_inc(qk_ready, 1)

            def project_v(u, i):
                if u.k < 2:
                    pe.wait_ge(w_low_done, 3)
                high, low = w_high[u.layer, "v"], w_low[u.layer, "v"]
                where = slice(i * P, (i + 1) * P)
                for k in range(CH):
                    for n, (r, w) in enumerate(((rowsT_low, high), (rowsT_high, low), (rowsT_high, high))):
                        mm = nc.tensor.matmul(misc_bank[V_BANK[i]][:, 0:H], r[:, k, where], w[:, k, :],
                                              start=(k == 0 and n == 0), stop=(k == CH - 1 and n == 2))
                mm.then_inc(v_ready, 1)

            def transpose_shares(u, g):
                pe.wait_ge(shares_done, u.count(GROUPS, g + 1))
                s = shares[:, (u.k * GROUPS + g) % 2, :, :].rearrange("p a b -> p (a b)")
                for q in range(TILES):
                    mm = nc.tensor.transpose(misc_bank[SHARES_BANK[g]][:, q * P:(q + 1) * P],
                                             s[:, q * P:(q + 1) * P], identity[:, :])
                mm.then_inc(sharesT_ready, 1)

            def project_out(u, i):
                pe.wait_ge(heads_split_done, u.count(GROUPS, GROUPS))
                if u.k < 2:
                    pe.wait_ge(w_low_done, 8)
                high, low = w_high[u.layer, "o"], w_low[u.layer, "o"]
                where = slice(i * P, (i + 1) * P)
                for k in range(CH):
                    for n, (r, w) in enumerate(((headsT_low, high), (headsT_high, low), (headsT_high, high))):
                        mm = nc.tensor.matmul(misc_bank[OUT_BANK[i]][:, 0:H], r[:, k, where], w[:, k, :],
                                              start=(k == 0 and n == 0), stop=(k == CH - 1 and n == 2))
                mm.then_inc(out_ready, 1)

            freed = {"rows": rows_low_done, "qk": qk_low_done, "v": values_done, "shares": sharesT_done,
                     "out": result_done}
            per_unit = {"rows": TILES, "qk": CH, "v": TILES, "shares": GROUPS, "out": TILES}
            users = [None, None]

            def take(bank, kind, u, i):
                if users[bank] is not None:
                    was, v, n = users[bank]
                    pe.wait_ge(freed[was], v.count(per_unit[was], n + 1))
                users[bank] = (kind, u, i)

            pe.wait_ge(constants_done, 3)

            def slot(attend, project, output, norm):
                if attend is not None and attend.turn is not None and attend.k == 3:
                    users[0], users[1] = ("v", attend, 1), ("shares", attend.before(1), 1)
                for step in range(HEADS):
                    if attend is not None:
                        scores(attend, step)
                    if project is not None and step == TRANSPOSE_ROWS_STEP:
                        for i in range(TILES):
                            take(ROWS_BANK[i], "rows", project, i)
                            transpose_rows(project, i)
                    if output is not None and step == SHARES_STEPS[2]:
                        take(SHARES_BANK[2], "shares", output, 2)
                        transpose_shares(output, 2)
                    if attend is not None:
                        for g in range(2):
                            if step == SHARES_STEPS[g]:
                                take(SHARES_BANK[g], "shares", attend, g)
                                transpose_shares(attend, g)
                    for c in range(CH):
                        for which in range(2):
                            if project is not None and step == QK_STEPS[c][which]:
                                if which == 0:
                                    take(QK_BANK[c], "qk", project, c)
                                project_qk(project, c, which)
                    for i in range(TILES):
                        if output is not None and step == OUT_STEPS[i]:
                            take(OUT_BANK[i], "out", output, i)
                            project_out(output, i)
                        if project is not None and step == V_STEPS[i]:
                            take(V_BANK[i], "v", project, i)
                            project_v(project, i)
                    if attend is not None and step >= 1:
                        transposes(attend, step - 1)
                    if output is not None and step == 0:
                        transposes(output, HEADS - 1)
                    if output is not None and step == VALUES_STEPS[2]:
                        weigh_values(output, 2)
                    if attend is not None:
                        for g in range(2):
                            if step == VALUES_STEPS[g]:
                                weigh_values(attend, g)

            program(slot, pe.Fori)


def kernel(x, adj, L0_gnn_Wq, L0_gnn_Wk, L0_gnn_Wv, L0_gnn_bv, L0_gnn_Wo, L0_gnn_bo,
           L1_gnn_Wq, L1_gnn_Wk, L1_gnn_Wv, L1_gnn_bv, L1_gnn_Wo, L1_gnn_bo):
    import numpy as np
    import concourse.bacc as bacc
    from concourse.bass_utils import run_bass_kernel_spmd

    nc = bacc.Bacc("TRN2", target_bir_lowering=False, num_devices=1)
    arrays = {"x": np.ascontiguousarray(x), "adj": np.ascontiguousarray(adj)}
    for l, ws in enumerate(((L0_gnn_Wq, L0_gnn_Wk, L0_gnn_Wv, L0_gnn_Wo), (L1_gnn_Wq, L1_gnn_Wk, L1_gnn_Wv, L1_gnn_Wo))):
        for n, w in zip("qkvo", ws):
            w = np.asarray(w).T
            if n in "qk":
                w = w.reshape(w.shape[0], 4, 3, 32).transpose(0, 2, 1, 3).reshape(w.shape)
            arrays[f"w{l}{n}"] = np.ascontiguousarray(w)
    for l, bs in enumerate(((L0_gnn_bv, L0_gnn_bo), (L1_gnn_bv, L1_gnn_bo))):
        for n, b in zip("vo", bs):
            arrays[f"b{l}{n}"] = np.ascontiguousarray(b)
    ins = {n: nc.dram_tensor(n, a.shape, F32, kind="ExternalInput").ap() for n, a in arrays.items()}
    out = nc.dram_tensor("out", arrays["x"].shape, F32, kind="ExternalOutput").ap()
    build(nc, ins["x"], ins["adj"], {(l, n): ins[f"w{l}{n}"] for l in range(2) for n in "qkvo"},
          {(l, n): ins[f"b{l}{n}"] for l in range(2) for n in "vo"}, out)
    r = run_bass_kernel_spmd(nc, [arrays], core_ids=[0])
    return r.results[0]["out"]
```

```python
from contextlib import ExitStack

import concourse.bass as bass
from concourse import mybir

F32 = mybir.dt.float32
F32R = mybir.dt.float32r
ALU = mybir.AluOpType
ACT = mybir.ActivationFunctionType
AX = mybir.AxisListType

P = 128
EPS = 1e-5
LARGEST = 3.4028234663852886e38
GROUP = 4
COPIES = 3

STEPS = 12
TENSOR = {
    "rows": (-12.0, -11.9),
    "queries": (-10.8, -8.8, -6.8),
    "keys": (-9.4, -7.4, -5.4),
    "v": (-2.8, -1.8),
    "scores": (-0.4, 0.6, 1.6, 2.6, 3.6, 4.6, 5.2, 5.6, 7.6, 8.6, 9.6, 10.6),
    "transposes": (1.5, 2.9, 3.5, 4.5, 5.5, 6.5, 7.5, 8.5, 9.5, 10.5, 11.5, 12.5),
    "values": (6.8, 10.8, 14.8),
    "shares": (7.6, 11.6, 15.6),
    "out": (19.4, 20.4),
}
SCALAR = {
    "rows_high": (-11.5, -11.4),
    "qk_high": (-10.1, -8.1, -6.1),
    "exp": (0.0, 1.0, 2.0, 3.0, 4.0, 5.0, 6.0, 7.0, 8.0, 9.0, 10.0, 11.0),
    "copy": {0: 1.3, 2: 3.3, 4: 5.3, 5: 6.3, 6: 7.3, 7: 8.3, 8: 9.3, 9: 10.3, 10: 11.3},
    "shares": (7.7, 11.7, 15.7),
}
VECTOR = {
    "statistics": (-14.7, -13.8),
    "mean": (-13.5, -13.4),
    "normalise": (-12.8, -12.7),
    "rows_low": (-10.9, -10.8),
    "qk_low": (-8.8, -6.8, -4.8),
    "v": (-2.2, -1.2),
    "negate": (0.0, 1.0, 2.0, 3.0, 4.0, 5.0, 6.0, 7.0, 8.0, 9.0, 10.0, 11.0),
    "copy": {1: 3.4, 3: 5.4, 11: 13.4},
    "share": (6.9, 10.9, 14.9),
    "scale": (8.4, 12.4, 16.4),
    "result": (20.6, 21.6),
}
POOL = {
    "deviation": (-14.7,),
    "bias": (-9.5,),
    "half": (0.0, 1.0, 2.0, 3.0, 4.0, 5.0, 6.0, 7.0, 8.0, 9.0, 10.0, 11.0),
    "rest": (3.9, 7.9, 11.9),
    "split": (8.8, 13.0, 16.8),
}
MISC = {"rows": (0, 1), "qk": (0, 1, 0), "out": (1, 0), "v": (1, 0)}


def when(plan, *names):
    calls = []
    for name in names:
        times = plan[name]
        for i, t in (times.items() if isinstance(times, dict) else enumerate(times)):
            calls.append((t % STEPS, name, i, int(t // STEPS) + 2))
    return [c[1:] for c in sorted(calls)]


ACT_COPIES, DVE_COPIES = len(SCALAR["copy"]), len(VECTOR["copy"])


def is_act_copy(head):
    return head in SCALAR["copy"]


class Unit:

    def __init__(self, k, turn=None, units=64):
        self.k, self.turn, self.units = k, turn, units
        first, last = k == 0, turn is None and k == units - 1
        self.layer = 0 if (k % 2 or first) and not last else 1
        self.t = 0 if first else units // 2 - 1 if last else (k + 1) // 2 if k % 2 else (k - 2) // 2

    def graph(self):
        return self.t if self.turn is None else self.turn * 2 + self.t

    def count(self, per_unit, done):
        c = self.k * per_unit + done
        return max(c, 0) if self.turn is None else self.turn * (4 * per_unit) + c

    def before(self, n):
        return Unit(self.k - n, self.turn, self.units)


def build(nc, x, adj, weights, biases, out):
    B, N, H = x.shape
    HEAD = 32
    HEADS = H // HEAD
    GROUPS = HEADS // GROUP
    CH = H // P
    TILES = N // P
    UNITS = 2 * B
    QUADS = P // HEAD
    ROW = CH * N
    SCALE = float(H) ** -0.5

    with ExitStack() as ctx:
        def sb(name, shape, dt=F32):
            return ctx.enter_context(nc.sbuf_tensor(name, shape, dt))

        def psum(name):
            return ctx.enter_context(nc.psum_tensor(name, [P, 512], F32))

        def sem(name):
            return ctx.enter_context(nc.semaphore(name))

        w_high = {(l, n): sb(f"w_high_{l}{n}", [P, CH, H], F32R) for l in range(2) for n in "qkvo"}
        w_low = {(l, n): sb(f"w_low_{l}{n}", [P, CH, H], F32R) for l in range(2) for n in "qkvo"}
        v_bias = [sb(f"v_bias{l}", [P, H]) for l in range(2)]
        o_bias = [sb(f"o_bias{l}", [P, H]) for l in range(2)]
        identity = sb("identity", [P, P])
        minus_half = sb("minus_half", [P, TILES])

        rows = [[sb(f"rows{l}{i}", [P, TILES, H]) for i in range(2)] for l in range(2)]
        bias = [sb(f"bias{i}", [P, TILES, N]) for i in range(4)]
        stats = sb("stats", [P, TILES, 6])
        mean_var = sb("mean_var", [P, TILES, 2])
        var_eps = sb("var_eps", [P, TILES])
        inv_dev = sb("inv_dev", [P, TILES])
        normed = sb("normed", [P, TILES, H])
        rowsT_high = [sb(f"rowsT_high{i}", [P, CH, N], F32R) for i in range(2)]
        rowsT_low = [sb(f"rowsT_low{i}", [P, CH, N], F32R) for i in range(2)]
        split_qk = sb("split_qk", [P, 4, ROW], F32R)
        stack = sb("stack", [COPIES * HEAD, QUADS, 2, ROW], F32R)
        values = [sb(f"values{i}", [P, TILES, H]) for i in range(2)]
        NEG, PROB, PROBT = 4, 4, 6
        neg = sb("neg", [P, NEG, TILES, N])
        prob = sb("prob", [P, PROB, TILES, N])
        probT = sb("probT", [P, PROBT, TILES, N])
        neg_max = [sb(f"neg_max{i}", [P, HEADS, TILES]) for i in range(2)]
        sums = [sb(f"sums{i}", [P, HEADS, TILES]) for i in range(2)]
        half = sb("half", [P, GROUP, TILES, N // 2])
        quarter = sb("quarter", [P, GROUP, TILES, N // 4])
        eighth = sb("eighth", [P, GROUP, TILES, N // 8])
        total = sb("total", [P, TILES, GROUP])
        nonzero = sb("nonzero", [P, TILES, GROUP])
        inverse = sb("inverse", [P, TILES, GROUP])
        shares = sb("shares", [P, 2, TILES * GROUP, HEAD])
        sharesT = sb("sharesT", [P, N])
        headsT = sb("headsT", [P, 2, N])
        headsT_high = sb("headsT_high", [P, GROUPS, N], F32R)
        headsT_low = sb("headsT_low", [P, GROUPS, N], F32R)

        score_bank = [psum(f"score_bank{i}") for i in range(2)]
        probT_bank = [psum(f"probT_bank{i}") for i in range(2)]
        values_bank = [psum(f"values_bank{i}") for i in range(2)]
        misc_bank = [psum(f"misc_bank{i}") for i in range(2)]

        staging = [neg[:, :, :, :].rearrange("p a b c -> p (a b c)")[:, 0:CH * H],
                   prob[:, :, :, :].rearrange("p a b c -> p (a b c)")[:, 0:CH * H],
                   probT[:, :, :, :].rearrange("p a b c -> p (a b c)")[:, 0:CH * H],
                   probT[:, :, :, :].rearrange("p a b c -> p (a b c)")[:, 3 * 512:3 * 512 + CH * H]]
        matrices = [(l, n) for l in range(2) for n in "qkvo"]

        passed = sem("passed")
        w_loaded = [sem(f"w_loaded{i}") for i in range(4)]
        bias_rows_loaded = sem("bias_rows_loaded")
        rows_loaded = [sem(f"rows_loaded{i}") for i in range(2)]
        bias_loaded = [sem(f"bias_loaded{i}") for i in range(4)]
        stacked = [sem(f"stacked{g}") for g in range(QUADS)]
        stored = [sem(f"stored{i}") for i in range(2)]
        w_high_done = sem("w_high_done")
        exp_done = sem("exp_done")
        rows_high_done = sem("rows_high_done")
        qk_high_done = sem("qk_high_done")
        sharesT_done = sem("sharesT_done")
        act_copy_done = sem("act_copy_done")
        w_low_done = sem("w_low_done")
        neg_done = sem("neg_done")
        rows_low_done = sem("rows_low_done")
        qk_low_done = sem("qk_low_done")
        values_done = sem("values_done")
        stats_done = sem("stats_done")
        mean_done = sem("mean_done")
        normed_done = sem("normed_done")
        heads_done = sem("heads_done")
        result_done = sem("result_done")
        guard_done = sem("guard_done")
        shares_done = sem("shares_done")
        dve_copy_done = sem("dve_copy_done")
        scores_done = sem("scores_done")
        probT_ready = sem("probT_ready")
        heads_ready = sem("heads_ready")
        rowsT_ready = sem("rowsT_ready")
        qk_ready = sem("qk_ready")
        v_ready = sem("v_ready")
        sharesT_ready = sem("sharesT_ready")
        out_ready = sem("out_ready")
        constants_done = sem("constants_done")
        half_done = sem("half_done")
        quarter_done = sem("quarter_done")
        eighth_done = sem("eighth_done")
        eps_done = sem("eps_done")
        inv_dev_done = sem("inv_dev_done")
        heads_high_done = sem("heads_high_done")
        heads_split_done = sem("heads_split_done")
        residual_done = sem("residual_done")

        def program(slot, loop):
            def u(k, turn=None):
                return Unit(k, turn, UNITS)
            slot(None, u(0), None, u(1))
            slot(u(0), u(1), None, None)
            slot(u(1), None, u(0), u(2))
            slot(None, u(2), u(1), u(3))
            slot(u(2), u(3), None, u(4))
            turns = (UNITS - 6) // 4
            with loop(0, turns) as turn:
                for k in range(3, 7):
                    slot(u(k, turn), u(k + 1, turn), u(k - 1, turn), u(k + 2, turn))
            for k in range(3 + 4 * turns, UNITS - 3):
                slot(u(k), u(k + 1), u(k - 1), u(k + 2))
            k = UNITS - 1
            slot(u(k - 2), u(k - 1), u(k - 3), None)
            slot(u(k - 1), None, u(k - 2), u(k))
            slot(None, u(k), u(k - 1), None)
            slot(u(k), None, None, None)
            slot(None, None, u(k), None)

        block = ctx.enter_context(nc.Block())

        def rows_of(u):
            return rows[u.layer][u.t % 2]

        @block.sync
        def _(sync):
            def load_weights(i):
                l, n = matrices[i]
                sync.dma_start(staging[i % 4].rearrange("p (c o) -> p c o", c=CH),
                               weights[l, n].rearrange("(c p) o -> p c o", p=P)).then_inc(w_loaded[i % 4], 16)

            def load_unit(u):
                sync.wait_ge(neg_done, u.before(4).count(2 * HEADS, 2 * HEADS))
                sync.dma_start(bias[u.k % 4][:, :, :],
                               adj[bass.ds(u.graph(), 1)].rearrange("a (i p) k -> p (a i) k", p=P)
                               ).then_inc(bias_loaded[u.k % 4], 16)
                if u.layer == 0:
                    sync.wait_ge(result_done, u.before(4 if u.k != 3 else 3).count(TILES, TILES))
                    sync.dma_start(rows_of(u)[:, :, :],
                                   x[bass.ds(u.graph(), 1)].rearrange("a (i p) c -> p (a i) c", p=P)
                                   ).then_inc(rows_loaded[u.t % 2], 16)

            def stack_quadrant(u, g):
                sync.wait_ge(scores_done, u.before(1).count(HEADS, CH * (g + 1)))
                quad = split_qk[g * HEAD:(g + 1) * HEAD, :, :].bitcast(F32)
                for part, (q, k) in enumerate(((1, 2), (1, 3), (0, 2))):
                    sync.dma_start(stack[part * HEAD:(part + 1) * HEAD, g, :, :].bitcast(F32),
                                   quad[:, q:k + 1:k - q, :]).then_inc(stacked[g], 16)

            load_weights(0)
            load_unit(Unit(0))
            load_weights(1)
            load_weights(2)
            load_weights(3)
            for l in range(2):
                for tile, name in ((v_bias, "v"), (o_bias, "o")):
                    sync.dma_start(tile[l][:, :], biases[l, name].rearrange("(a c) -> a c", a=1).to_broadcast([P, H])
                                   ).then_inc(bias_rows_loaded, 16)
            load_unit(Unit(1))
            for i in range(4, 8):
                sync.wait_ge(w_low_done, i - 3)
                load_weights(i)

            def slot(attend, project, output, norm):
                if norm is not None and norm.k > 1:
                    load_unit(norm)
                if project is not None:
                    sync.wait_ge(qk_low_done, project.count(CH, CH))
                    sync.sem_inc(passed, 1)
                    for g in range(QUADS - 1):
                        stack_quadrant(project, g)
                if output is not None and output.layer == 1:
                    sync.wait_ge(result_done, output.count(TILES, TILES))
                    sync.dma_start(out[bass.ds(output.graph(), 1)].rearrange("a (i p) c -> p (a i) c", p=P),
                                   rows_of(output)[:, :, :]).then_inc(stored[output.t % 2], 16)
                if project is not None:
                    stack_quadrant(project, QUADS - 1)

            program(slot, sync.Fori)
            for i in range(2):
                sync.wait_ge(stored[i], 16 * (B // 2))

        @block.gpsimd
        def _(pool):
            nc.gpsimd.memset(identity[:, :], 0.0).then_inc(constants_done, 1)
            nc.gpsimd.memset(minus_half[:, :], -0.5).then_inc(constants_done, 1)
            pool.wait_ge(constants_done, 2)
            nc.gpsimd.affine_select(out=identity[:, :], in_=identity[:, :], compare_op=ALU.not_equal, fill=1.0,
                                    base=0, pattern=[[-1, P]], channel_multiplier=1).then_inc(constants_done, 1)

            def invert_deviation(u):
                pool.wait_ge(mean_done, u.count(TILES, TILES))
                pool.sem_inc(passed, 1)
                nc.gpsimd.tensor_scalar(var_eps[:, :], mean_var[:, :, 1], EPS, None, ALU.add).then_inc(eps_done, 1)
                pool.wait_ge(eps_done, u.count(1, 1))
                nc.gpsimd.tensor_tensor(inv_dev[:, :], var_eps[:, :], minus_half[:, :], ALU.pow
                                        ).then_inc(inv_dev_done, 1)

            def add_half(u, step):
                pool.wait_ge(neg_done, u.count(2 * HEADS, 2 * step + 2))
                n = neg[:, step % NEG, :, :]
                nc.gpsimd.tensor_tensor(half[:, step % GROUP, :, :], n[:, :, 0:N // 2], n[:, :, N // 2:N], ALU.add
                                        ).then_inc(half_done, 1)

            def add_rest(u, g):
                pool.wait_ge(half_done, u.count(HEADS, GROUP * (g + 1)))
                nc.gpsimd.tensor_tensor(quarter[:, :, :, :], half[:, :, :, 0:N // 4], half[:, :, :, N // 4:N // 2],
                                        ALU.add).then_inc(quarter_done, 1)
                pool.wait_ge(quarter_done, u.count(GROUPS, g + 1))
                pool.wait_ge(guard_done, u.count(3 * GROUPS, 3 * g))
                nc.gpsimd.tensor_tensor(eighth[:, :, :, :], quarter[:, :, :, 0:N // 8], quarter[:, :, :, N // 8:N // 4],
                                        ALU.add).then_inc(eighth_done, 1)

            def split_heads(u, g):
                i = (u.k * GROUPS + g) % 2
                if g == 0:
                    pool.wait_ge(out_ready, u.before(1).count(TILES, TILES))
                pool.wait_ge(heads_done, u.count(GROUPS, g + 1))
                pool.sem_inc(passed, 1)
                nc.gpsimd.tensor_scalar(headsT_high[:, g, :], headsT[:, i, :], 1.0, 0.0, ALU.mult, ALU.add
                                        ).then_inc(heads_high_done, 1)
                pool.wait_ge(heads_high_done, u.count(GROUPS, g + 1))
                nc.gpsimd.tensor_tensor(headsT_low[:, g, :], headsT[:, i, :], headsT_high[:, g, :].bitcast(F32),
                                        ALU.subtract).then_inc(heads_split_done, 1)

            def add_output_bias(u):
                if u.k == 0:
                    pool.wait_ge(bias_rows_loaded, 16 * 4)
                pool.wait_ge(normed_done, u.count(TILES, TILES))
                r = rows_of(u)
                for i in range(TILES):
                    add = nc.gpsimd.tensor_tensor(r[:, i, :], r[:, i, :], o_bias[u.layer][:, :], ALU.add)
                add.then_inc(residual_done, 1)

            invert_deviation(Unit(0))
            calls = {"deviation": lambda u, i: invert_deviation(u), "bias": lambda u, i: add_output_bias(u),
                     "half": add_half, "rest": add_rest, "split": split_heads}

            def slot(attend, project, output, norm):
                for name, i, role in when(POOL, *calls):
                    u = (norm, project, attend, output)[role]
                    if u is not None and (name != "deviation" or u.k > 0):
                        calls[name](u, i)

            program(slot, pool.Fori)

        @block.scalar
        def _(act):
            for i, (l, n) in enumerate(matrices):
                act.wait_ge(w_loaded[i % 4], 16 * (i // 4 + 1))
                scale = (SCALE / 2 if l == 0 else SCALE) if n == "q" else 1.0
                nc.scalar.activation(w_high[l, n][:, :, :].rearrange("p c o -> p (c o)"), staging[i % 4], ACT.Copy,
                                     scale=scale).then_inc(w_high_done, 1)

            def exps(u, step):
                act.wait_ge(probT_ready, u.count(HEADS, step + 1 - PROB))
                for q in range(TILES):
                    act.wait_ge(neg_done, u.count(2 * HEADS, 2 * step + q + 1))
                    nc.scalar.activation(prob[:, step % PROB, q, :], neg[:, step % NEG, q, :], ACT.Exp, scale=-1.0,
                                         bias=neg_max[u.k % 2][:, step, q:q + 1],
                                         accum_out=sums[u.k % 2][:, step, q:q + 1]).then_inc(exp_done, 1)

            def copy_probT(u, step):
                n = sum(is_act_copy(s) for s in range(step))
                act.wait_ge(probT_ready, u.count(HEADS, step + 1))
                act.wait_ge(heads_ready, u.count(GROUPS, (step - PROBT) // GROUP + 1))
                nc.scalar.activation(probT[:, step % PROBT, :, :].rearrange("p a b -> p (a b)"),
                                     probT_bank[step % 2][:, :], ACT.Copy).then_inc(act_copy_done, 1)

            def rows_high(u, i):
                act.wait_ge(rowsT_ready, u.count(TILES, i + 1))
                act.wait_ge(v_ready, u.before(1).count(TILES, 0))
                act.wait_ge(qk_ready, u.before(1).count(CH, 0))
                nc.scalar.activation(rowsT_high[u.k % 2][:, :, i * P:(i + 1) * P],
                                     misc_bank[MISC["rows"][i]][:, 0:H].rearrange("p (c t) -> p c t", c=CH), ACT.Relu
                                     ).then_inc(rows_high_done, 1)

            def qk_high(u, c):
                act.wait_ge(qk_ready, u.count(CH, c + 1))
                if c == 0:
                    for g in range(QUADS):
                        act.wait_ge(stacked[g], u.count(16 * COPIES, 0))
                nc.scalar.activation(split_qk[:, 1:3, c * N:(c + 1) * N],
                                     misc_bank[MISC["qk"][c]][:, :].rearrange("p (a n) -> p a n", a=2), ACT.Copy
                                     ).then_inc(qk_high_done, 1)

            def copy_sharesT(u, g):
                act.wait_ge(sharesT_ready, u.count(GROUPS, g + 1))
                act.wait_ge(heads_done, u.count(GROUPS, g))
                nc.scalar.activation(sharesT[:, :], values_bank[(u.k * GROUPS + g) % 2][:, N:2 * N], ACT.Copy
                                     ).then_inc(sharesT_done, 1)

            calls = {"rows_high": rows_high, "qk_high": qk_high, "exp": exps, "copy": copy_probT,
                     "shares": copy_sharesT}

            def slot(attend, project, output, norm):
                for name, i, role in when(SCALAR, *calls):
                    u = (norm, project, attend, output)[role]
                    if u is not None:
                        calls[name](u, i)

            program(slot, act.Fori)

        @block.vector
        def _(dve):
            def statistics(u, i):
                if u.layer == 0:
                    dve.wait_ge(rows_loaded[u.t % 2], rows_count(u))
                else:
                    dve.wait_ge(result_done, before_layer(u).count(TILES, i + 1))
                nc.vector.bn_stats(stats[:, i, :], rows_of(u)[:, i, :]).then_inc(stats_done, 1)

            def rows_count(u):
                return 16 * (u.t // 2 + 1) if u.turn is None else u.turn * 16 + 16 * (u.t // 2 + 1)

            def bias_count(u):
                return 16 * (u.k // 4 + 1) if u.turn is None else u.turn * 16 + 16 * (u.k // 4 + 1)

            def before_layer(u):
                k = max(2 * u.t - 1, 0)
                return Unit(k, u.turn, UNITS)

            def mean(u, i):
                dve.wait_ge(stats_done, u.count(TILES, i + 1))
                dve.wait_ge(eps_done, u.count(1, 0))
                dve.sem_inc(passed, 1)
                nc.vector.bn_aggr(mean_var[:, i, :], stats[:, i, :]).then_inc(mean_done, 1)

            def normalise(u, i):
                dve.wait_ge(inv_dev_done, u.count(1, 1))
                dve.wait_ge(rowsT_ready, u.count(TILES, 0))
                nc.vector.tensor_scalar(normed[:, i, :], rows_of(u)[:, i, :], mean_var[:, i, 0:1], inv_dev[:, i:i + 1],
                                        ALU.subtract, ALU.mult).then_inc(normed_done, 1)

            def rows_low(u, i):
                dve.wait_ge(rows_high_done, u.count(TILES, i + 1))
                where = slice(i * P, (i + 1) * P)
                nc.vector.scalar_tensor_tensor(
                    out=rowsT_low[u.k % 2][:, :, where], in0=misc_bank[MISC["rows"][i]][:, 0:H].rearrange("p (c t) -> p c t", c=CH),
                    scalar=0.0, in1=rowsT_high[u.k % 2][:, :, where].bitcast(F32), op0=ALU.max, op1=ALU.subtract
                ).then_inc(rows_low_done, 1)

            def qk_low(u, c):
                dve.wait_ge(qk_high_done, u.count(CH, c + 1))
                where = slice(c * N, (c + 1) * N)
                nc.vector.tensor_tensor(split_qk[:, 0:4:3, where],
                                        misc_bank[MISC["qk"][c]][:, :].rearrange("p (a n) -> p a n", a=2),
                                        split_qk[:, 1:3, where].bitcast(F32), ALU.subtract).then_inc(qk_low_done, 1)

            def add_value_bias(u, i):
                dve.wait_ge(v_ready, u.count(TILES, i + 1))
                dve.wait_ge(heads_ready, u.before(1).count(GROUPS, 0))
                nc.vector.tensor_tensor(values[u.k % 2][:, i, :], misc_bank[MISC["v"][i]][:, 0:H], v_bias[u.layer][:, :],
                                        ALU.add).then_inc(values_done, 1)

            def negate_scores(u, step):
                if step == 0:
                    dve.wait_ge(bias_loaded[u.k % 4], bias_count(u))
                dve.wait_ge(scores_done, u.count(HEADS, step + 1))
                dve.wait_ge(exp_done, u.count(2 * HEADS, 2 * (step + 1 - NEG)))
                dve.wait_ge(half_done, u.count(HEADS, step + 1 - NEG))
                dve.sem_inc(passed, 1)
                for q in range(TILES):
                    nc.vector.tensor_tensor_reduce(
                        out=neg[:, step % NEG, q, :], in0=score_bank[step % 2][:, q * N:(q + 1) * N],
                        in1=bias[u.k % 4][:, q, :], scale=-2.0 if u.layer == 0 else -1.0, scalar=LARGEST,
                        op0=ALU.add, op1=ALU.min, accum_out=neg_max[u.k % 2][:, step, q:q + 1]
                    ).then_inc(neg_done, 1)

            def copy_probT(u, step):
                dve.wait_ge(probT_ready, u.count(HEADS, step + 1))
                dve.wait_ge(heads_ready, u.count(GROUPS, (step - PROBT) // GROUP + 1))
                nc.vector.tensor_copy(probT[:, step % PROBT, :, :].rearrange("p a b -> p (a b)"),
                                      probT_bank[step % 2][:, :]).then_inc(dve_copy_done, 1)

            def share(u, g):
                heads = slice(GROUP * g, GROUP * (g + 1))
                dve.wait_ge(exp_done, u.count(2 * HEADS, 2 * GROUP * (g + 1)))
                nc.vector.reciprocal(inverse[:, :, :], sums[u.k % 2][:, heads, :].rearrange("p h q -> p q h")).then_inc(guard_done, 1)
                dve.wait_ge(eighth_done, u.count(GROUPS, g + 1))
                nc.vector.tensor_reduce(total[:, :, :].rearrange("p q h -> p h q"), eighth[:, :, :, :], AX.X, ALU.add).then_inc(guard_done, 1)
                dve.wait_ge(guard_done, u.count(3 * GROUPS, 3 * g + 2))
                nc.vector.scalar_tensor_tensor(out=nonzero[:, :, :], in0=total[:, :, :], scalar=-1.0,
                                               in1=neg_max[u.k % 2][:, heads, :].rearrange("p h q -> p q h"), op0=ALU.mult, op1=ALU.min
                                               ).then_inc(guard_done, 1)
                dve.wait_ge(guard_done, u.count(3 * GROUPS, 3 * g + 3))
                wide = [t[:, :, :].rearrange("p q (h a) -> p (q h) a", a=1).to_broadcast([P, TILES * GROUP, HEAD])
                        for t in (nonzero, inverse)]
                nc.vector.scalar_tensor_tensor(out=shares[:, (u.k * GROUPS + g) % 2, :, :], in0=wide[0],
                                               scalar=0.0, in1=wide[1], op0=ALU.not_equal, op1=ALU.mult
                                               ).then_inc(shares_done, 1)

            def scale_heads(u, g):
                i = (u.k * GROUPS + g) % 2
                dve.wait_ge(heads_ready, u.count(GROUPS, g + 1))
                dve.wait_ge(sharesT_done, u.count(GROUPS, g + 1))
                dve.wait_ge(heads_split_done, u.count(GROUPS, g - 1))
                nc.vector.tensor_tensor(headsT[:, i, :], values_bank[i][:, 0:N], sharesT[:, :], ALU.mult
                                        ).then_inc(heads_done, 1)

            def result(u, i):
                dve.wait_ge(out_ready, u.count(TILES, i + 1))
                dve.wait_ge(residual_done, u.count(1, 1))
                to = rows[1][u.t % 2]
                if u.layer == 0 and i == 0:
                    dve.wait_ge(stored[u.t % 2], stored_count(u))
                nc.vector.tensor_tensor(to[:, i, :], misc_bank[MISC["out"][i]][:, 0:H], rows_of(u)[:, i, :], ALU.add
                                        ).then_inc(result_done, 1)

            def stored_count(u):
                return 16 * (u.t // 2) if u.turn is None else u.turn * 16 + 16 * (u.t // 2)

            def split_low(i):
                l, n = matrices[i]
                dve.wait_ge(w_high_done, i + 1)
                scale = (SCALE / 2 if l == 0 else SCALE) if n == "q" else 1.0
                nc.vector.scalar_tensor_tensor(
                    out=w_low[l, n][:, :, :].rearrange("p c o -> p (c o)"), in0=staging[i % 4], scalar=scale,
                    in1=w_high[l, n][:, :, :].rearrange("p c o -> p (c o)").bitcast(F32), op0=ALU.mult, op1=ALU.subtract
                ).then_inc(w_low_done, 1)

            for i in range(TILES):
                statistics(Unit(0), i)
            for i in range(TILES):
                mean(Unit(0), i)
            for i in range(3):
                split_low(i)
            for i in range(TILES):
                normalise(Unit(0), i)
            for i in range(3, 8):
                split_low(i)
            dve.wait_ge(bias_rows_loaded, 16 * 4)

            calls = {"statistics": statistics, "mean": mean, "normalise": normalise, "rows_low": rows_low,
                     "qk_low": qk_low, "v": add_value_bias, "negate": negate_scores, "copy": copy_probT,
                     "share": share, "scale": scale_heads, "result": result}

            def slot(attend, project, output, norm):
                for name, i, role in when(VECTOR, *calls):
                    u = (norm, project, attend, output)[role]
                    if u is not None and (name not in ("statistics", "mean", "normalise") or u.k > 0):
                        calls[name](u, i)

            program(slot, dve.Fori)

        @block.tensor
        def _(pe):
            def copied(u, steps):
                n = sum(is_act_copy(s) for s in range(steps))
                return n, steps - n

            def scores(u, step):
                g, c = step // CH, step % CH
                if c == 0:
                    pe.wait_ge(stacked[g], u.count(16 * COPIES, 16 * COPIES))
                pe.wait_ge(neg_done, u.count(2 * HEADS, 2 * (step - 1)))
                for q in range(TILES):
                    mm = nc.tensor.matmul(score_bank[step % 2][:, q * N:(q + 1) * N],
                                          stack[:, g, 0, c * N + q * P:c * N + (q + 1) * P],
                                          stack[:, g, 1, c * N:(c + 1) * N], start=True, stop=True)
                mm.then_inc(scores_done, 1)

            def transposes(u, step):
                pe.wait_ge(exp_done, u.count(2 * HEADS, 2 * (step + 1)))
                if step >= 2:
                    n = sum(is_act_copy(s) for s in range(step - 1))
                    pe.wait_ge(act_copy_done, u.count(ACT_COPIES, n))
                    pe.wait_ge(dve_copy_done, u.count(DVE_COPIES, step - 1 - n))
                else:
                    n = sum(is_act_copy(s) for s in range(HEADS + step - 1))
                    pe.wait_ge(act_copy_done, u.before(1).count(ACT_COPIES, n))
                    pe.wait_ge(dve_copy_done, u.before(1).count(DVE_COPIES, HEADS + step - 1 - n))
                for k in range(TILES):
                    for q in range(TILES):
                        mm = nc.tensor.transpose(probT_bank[step % 2][:, k * N + q * P:k * N + (q + 1) * P],
                                                 prob[:, step % PROB, q, k * P:(k + 1) * P], identity[:, :])
                mm.then_inc(probT_ready, 1)

            def weigh_values(u, g):
                i = (u.k * GROUPS + g) % 2
                n = sum(is_act_copy(s) for s in range(GROUP * (g + 1)))
                pe.wait_ge(act_copy_done, u.count(ACT_COPIES, n))
                pe.wait_ge(dve_copy_done, u.count(DVE_COPIES, GROUP * (g + 1) - n))
                if g == 0:
                    pe.wait_ge(values_done, u.count(TILES, TILES))
                pe.wait_ge(heads_done, u.count(GROUPS, g - 1))
                for k in range(TILES):
                    for a in range(GROUP):
                        h = GROUP * g + a
                        mm = nc.tensor.matmul(values_bank[i][a * HEAD:(a + 1) * HEAD, 0:N],
                                              values[u.k % 2][:, k, h * HEAD:(h + 1) * HEAD],
                                              probT[:, h % PROBT, k, :], start=(k == 0), stop=(k == TILES - 1))
                mm.then_inc(heads_ready, 1)

            def transpose_rows(u, i):
                pe.wait_ge(normed_done, u.count(TILES, i + 1))
                for c in range(CH):
                    mm = nc.tensor.transpose(misc_bank[MISC["rows"][i]][:, c * P:(c + 1) * P],
                                             normed[:, i, c * P:(c + 1) * P], identity[:, :])
                mm.then_inc(rowsT_ready, 1)

            def project_qk(u, c, which):
                if which == 0 and c == 0:
                    pe.wait_ge(rows_low_done, u.count(TILES, TILES))
                    if u.k < 2:
                        pe.wait_ge(w_low_done, 2)
                high, low = w_high[u.layer, "qk"[which]], w_low[u.layer, "qk"[which]]
                r_high, r_low = rowsT_high[u.k % 2], rowsT_low[u.k % 2]
                cols = slice(c * P, (c + 1) * P)
                into = misc_bank[MISC["qk"][c]][:, which * N:(which + 1) * N]
                for k in range(CH):
                    for n, (w, r) in enumerate(((low, r_high), (high, r_low), (high, r_high))):
                        mm = nc.tensor.matmul(into, w[:, k, cols], r[:, k, :], start=(k == 0 and n == 0),
                                              stop=(k == CH - 1 and n == 2))
                if which == 1:
                    mm.then_inc(qk_ready, 1)

            def project_v(u, i):
                if u.k < 2:
                    pe.wait_ge(w_low_done, 3)
                high, low = w_high[u.layer, "v"], w_low[u.layer, "v"]
                r_high, r_low = rowsT_high[u.k % 2], rowsT_low[u.k % 2]
                where = slice(i * P, (i + 1) * P)
                for k in range(CH):
                    for n, (r, w) in enumerate(((r_low, high), (r_high, low), (r_high, high))):
                        mm = nc.tensor.matmul(misc_bank[MISC["v"][i]][:, 0:H], r[:, k, where], w[:, k, :],
                                              start=(k == 0 and n == 0), stop=(k == CH - 1 and n == 2))
                mm.then_inc(v_ready, 1)

            def transpose_shares(u, g):
                pe.wait_ge(shares_done, u.count(GROUPS, g + 1))
                s = shares[:, (u.k * GROUPS + g) % 2, :, :].rearrange("p a b -> p (a b)")
                for q in range(TILES):
                    mm = nc.tensor.transpose(values_bank[(u.k * GROUPS + g) % 2][:, N + q * P:N + (q + 1) * P],
                                             s[:, q * P:(q + 1) * P], identity[:, :])
                mm.then_inc(sharesT_ready, 1)

            def project_out(u, i):
                pe.wait_ge(heads_split_done, u.count(GROUPS, GROUPS))
                if u.k < 2:
                    pe.wait_ge(w_low_done, 8)
                high, low = w_high[u.layer, "o"], w_low[u.layer, "o"]
                where = slice(i * P, (i + 1) * P)
                for k in range(CH):
                    for n, (r, w) in enumerate(((headsT_low, high), (headsT_high, low), (headsT_high, high))):
                        mm = nc.tensor.matmul(misc_bank[MISC["out"][i]][:, 0:H], r[:, k, where], w[:, k, :],
                                              start=(k == 0 and n == 0), stop=(k == CH - 1 and n == 2))
                mm.then_inc(out_ready, 1)

            freed = {"rows": (rows_low_done, TILES), "qk": (qk_low_done, CH), "v": (values_done, TILES),
                     "out": (result_done, TILES)}
            last = [None, None]

            def take(kind, u, i):
                bank = MISC[kind][i]
                if last[bank] is not None:
                    was, v, n = last[bank]
                    pe.wait_ge(freed[was][0], v.count(freed[was][1], n + 1))
                last[bank] = (kind, u, i)

            pe.wait_ge(constants_done, 3)
            calls = {"rows": transpose_rows, "queries": lambda u, c: project_qk(u, c, 0),
                     "keys": lambda u, c: project_qk(u, c, 1), "v": project_v, "scores": scores,
                     "transposes": transposes, "values": weigh_values, "shares": transpose_shares, "out": project_out}
            takes = {"rows": "rows", "queries": "qk", "v": "v", "out": "out"}

            def slot(attend, project, output, norm):
                order = when(TENSOR, *calls)
                if attend is not None and attend.turn is not None and attend.k == 3:
                    for name, i, role in order:
                        if name in takes:
                            unit = attend.before(role - 1)
                            last[MISC[takes[name]][i]] = (takes[name], unit, i)
                for name, i, role in order:
                    u = (norm, project, attend, output)[role]
                    if u is not None:
                        if name in takes:
                            take(takes[name], u, i)
                        calls[name](u, i)

            program(slot, pe.Fori)


def kernel(x, adj, L0_gnn_Wq, L0_gnn_Wk, L0_gnn_Wv, L0_gnn_bv, L0_gnn_Wo, L0_gnn_bo,
           L1_gnn_Wq, L1_gnn_Wk, L1_gnn_Wv, L1_gnn_bv, L1_gnn_Wo, L1_gnn_bo):
    import numpy as np
    import concourse.bacc as bacc
    from concourse.bass_utils import run_bass_kernel_spmd

    nc = bacc.Bacc("TRN2", target_bir_lowering=False, num_devices=1)
    arrays = {"x": np.ascontiguousarray(x), "adj": np.ascontiguousarray(adj)}
    for l, ws in enumerate(((L0_gnn_Wq, L0_gnn_Wk, L0_gnn_Wv, L0_gnn_Wo), (L1_gnn_Wq, L1_gnn_Wk, L1_gnn_Wv, L1_gnn_Wo))):
        for n, w in zip("qkvo", ws):
            w = np.asarray(w).T
            if n in "qk":
                w = w.reshape(w.shape[0], 4, 3, 32).transpose(0, 2, 1, 3).reshape(w.shape)
            arrays[f"w{l}{n}"] = np.ascontiguousarray(w)
    for l, bs in enumerate(((L0_gnn_bv, L0_gnn_bo), (L1_gnn_bv, L1_gnn_bo))):
        for n, b in zip("vo", bs):
            arrays[f"b{l}{n}"] = np.ascontiguousarray(b)
    ins = {n: nc.dram_tensor(n, a.shape, F32, kind="ExternalInput").ap() for n, a in arrays.items()}
    out = nc.dram_tensor("out", arrays["x"].shape, F32, kind="ExternalOutput").ap()
    build(nc, ins["x"], ins["adj"], {(l, n): ins[f"w{l}{n}"] for l in range(2) for n in "qkvo"},
          {(l, n): ins[f"b{l}{n}"] for l in range(2) for n in "vo"}, out)
    r = run_bass_kernel_spmd(nc, [arrays], core_ids=[0])
    return r.results[0]["out"]
```

```python
from contextlib import ExitStack

import concourse.bass as bass
from concourse import mybir

F32 = mybir.dt.float32
F32R = mybir.dt.float32r
ALU = mybir.AluOpType
ACT = mybir.ActivationFunctionType
AX = mybir.AxisListType

P = 128
EPS = 1e-5
LARGEST = 3.4028234663852886e38
GROUP = 4
COPIES = 3

DVE_COPY_HEADS = (1, 2)
MISC = {"rows": (0, 1), "qk": (0, 1, 0), "out": (1, 1), "v": (0, 1)}


class Unit:

    def __init__(self, k, turn, units):
        self.k, self.turn, self.units = k, turn, units
        start = (0, 0), (0, 1), (0, 2), (1, 0)
        end = (0, units // 2 - 1), (1, units // 2 - 3), (1, units // 2 - 2), (1, units // 2 - 1)
        if turn is None and 0 <= k < 4:
            self.layer, self.t = start[k]
        elif turn is None and k >= units - 4:
            self.layer, self.t = end[k - (units - 4)]
        else:
            self.layer, self.t = (0, (k + 1) // 2) if k % 2 else (1, k // 2 - 1)
        self.own_rows = turn is None and self.t in (2, units // 2 - 1)

    def layer_before(self):
        if self.turn is not None or 3 <= self.t < self.units // 2 - 1:
            return Unit(2 * self.t - 1, self.turn, self.units)
        return Unit(self.t if self.t < 3 else self.units - 4, None, self.units)

    def graph(self):
        return self.t if self.turn is None else self.turn * 2 + self.t

    def count(self, per_unit, done):
        c = self.k * per_unit + done
        return max(c, 0) if self.turn is None else self.turn * (4 * per_unit) + c

    def before(self, n):
        return Unit(self.k - n, self.turn, self.units)


def build(nc, x, adj, weights, biases, out):
    B, N, H = x.shape
    HEAD = 32
    HEADS = H // HEAD
    GROUPS = HEADS // GROUP
    CH = H // P
    TILES = N // P
    UNITS = 2 * B
    LOOPED = 8
    TURNS = (UNITS - 6 - LOOPED) // 4
    QUADS = P // HEAD
    DVE_COPIES = len(DVE_COPY_HEADS)
    ACT_COPIES = HEADS - DVE_COPIES
    ROW = CH * N
    SCALE = float(H) ** -0.5

    with ExitStack() as ctx:
        def sb(name, shape, dt=F32):
            return ctx.enter_context(nc.sbuf_tensor(name, shape, dt))

        def psum(name):
            return ctx.enter_context(nc.psum_tensor(name, [P, 512], F32))

        def sem(name):
            return ctx.enter_context(nc.semaphore(name))

        w_high = {(l, n): sb(f"w_high_{l}{n}", [P, CH, H], F32R) for l in range(2) for n in "qkvo"}
        w_low = {(l, n): sb(f"w_low_{l}{n}", [P, CH, H], F32R) for l in range(2) for n in "qkvo"}
        v_bias = [sb(f"v_bias{l}", [P, H]) for l in range(2)]
        o_bias = [sb(f"o_bias{l}", [P, H]) for l in range(2)]
        identity = sb("identity", [P, P])
        minus_half = sb("minus_half", [P, TILES])

        rows = [[sb(f"rows{l}{i}", [P, TILES, H]) for i in range(2)] for l in range(2)]
        own_rows = sb("own_rows", [P, TILES, H])
        bias = [sb(f"bias{i}", [P, TILES, N]) for i in range(4)]
        stats = sb("stats", [P, TILES, 6])
        mean_var = sb("mean_var", [P, TILES, 2])
        var_eps = sb("var_eps", [P, TILES])
        inv_dev = sb("inv_dev", [P, TILES])
        normed = sb("normed", [P, TILES, H])
        rowsT_high = [sb(f"rowsT_high{i}", [P, CH, N], F32R) for i in range(2)]
        rowsT_low = [sb(f"rowsT_low{i}", [P, CH, N], F32R) for i in range(2)]
        split_qk = sb("split_qk", [P, 4, ROW], F32R)
        stack = sb("stack", [COPIES * HEAD, QUADS, 2, ROW], F32R)
        values = [sb(f"values{i}", [P, TILES, H]) for i in range(2)]
        NEG, PROB, PROBT = 4, 4, 6
        neg = sb("neg", [P, NEG, TILES, N])
        prob = sb("prob", [P, PROB, TILES, N])
        probT = sb("probT", [P, PROBT, TILES, N])
        neg_max = [sb(f"neg_max{i}", [P, HEADS, TILES]) for i in range(2)]
        sums = [sb(f"sums{i}", [P, HEADS, TILES]) for i in range(2)]
        half = sb("half", [P, GROUP, TILES, N // 2])
        quarter = sb("quarter", [P, GROUP, TILES, N // 4])
        eighth = sb("eighth", [P, GROUP, TILES, N // 8])
        total = sb("total", [P, TILES, GROUP])
        nonzero = [sb(f"nonzero{i}", [P, TILES, GROUP]) for i in range(2)]
        inverse = [sb(f"inverse{i}", [P, TILES, GROUP]) for i in range(2)]
        shares = sb("shares", [P, 2, TILES * GROUP, HEAD])
        sharesT = sb("sharesT", [P, N])
        headsT = sb("headsT", [P, 2, N])
        headsT_high = sb("headsT_high", [P, GROUPS, N], F32R)
        headsT_low = sb("headsT_low", [P, GROUPS, N], F32R)

        score_bank = [psum(f"score_bank{i}") for i in range(2)]
        probT_bank = [psum(f"probT_bank{i}") for i in range(2)]
        values_bank = [psum(f"values_bank{i}") for i in range(2)]
        misc_bank = [psum(f"misc_bank{i}") for i in range(2)]

        staging = [neg[:, :, :, :].rearrange("p a b c -> p (a b c)")[:, 0:CH * H],
                   prob[:, :, :, :].rearrange("p a b c -> p (a b c)")[:, 0:CH * H],
                   probT[:, :, :, :].rearrange("p a b c -> p (a b c)")[:, 0:CH * H],
                   probT[:, :, :, :].rearrange("p a b c -> p (a b c)")[:, 3 * 512:3 * 512 + CH * H]]
        matrices = [(l, n) for l in range(2) for n in "qkvo"]

        passed = sem("passed")
        w_loaded = [sem(f"w_loaded{i}") for i in range(4)]
        bias_rows_loaded = sem("bias_rows_loaded")
        rows_loaded = [sem(f"rows_loaded{i}") for i in range(2)]
        own_rows_loaded = sem("own_rows_loaded")
        bias_loaded = [sem(f"bias_loaded{i}") for i in range(4)]
        stacked = [sem(f"stacked{g}") for g in range(QUADS)]
        stored = [sem(f"stored{i}") for i in range(2)]
        w_high_done = sem("w_high_done")
        exp_done = sem("exp_done")
        rows_high_done = sem("rows_high_done")
        qk_high_done = sem("qk_high_done")
        sharesT_done = sem("sharesT_done")
        act_copy_done = sem("act_copy_done")
        w_low_done = sem("w_low_done")
        neg_done = sem("neg_done")
        rows_low_done = sem("rows_low_done")
        qk_low_done = sem("qk_low_done")
        values_done = sem("values_done")
        stats_done = sem("stats_done")
        mean_done = sem("mean_done")
        normed_done = sem("normed_done")
        heads_done = sem("heads_done")
        result_done = sem("result_done")
        guard_done = sem("guard_done")
        shares_done = sem("shares_done")
        dve_copy_done = sem("dve_copy_done")
        scores_done = sem("scores_done")
        probT_ready = sem("probT_ready")
        heads_ready = sem("heads_ready")
        rowsT_ready = sem("rowsT_ready")
        qk_ready = sem("qk_ready")
        v_ready = sem("v_ready")
        sharesT_ready = sem("sharesT_ready")
        out_ready = sem("out_ready")
        constants_done = sem("constants_done")
        half_done = sem("half_done")
        quarter_done = sem("quarter_done")
        eighth_done = sem("eighth_done")
        eps_done = sem("eps_done")
        vo_low_done = sem("vo_low_done")
        inv_dev_done = sem("inv_dev_done")
        heads_high_done = sem("heads_high_done")
        heads_split_done = sem("heads_split_done")
        residual_done = sem("residual_done")

        def program(slot, loop):
            def u(k, turn=None):
                return Unit(k, turn, UNITS) if 0 <= k < UNITS else None

            def side_by_side(k, turn=None):
                slot(u(k, turn), u(k + 1, turn), u(k - 1, turn), u(k + 2, turn))

            for k in range(-2, LOOPED):
                side_by_side(k)
            with loop(0, TURNS) as turn:
                for k in range(LOOPED, LOOPED + 4):
                    side_by_side(k, turn)
            for k in range(LOOPED + 4 * TURNS, UNITS + 1):
                side_by_side(k)

        block = ctx.enter_context(nc.Block())

        def rows_of(u):
            return own_rows if u.own_rows else rows[u.layer][u.t % 2]

        @block.sync
        def _(sync):
            def load_weights(i):
                l, n = matrices[i]
                sync.dma_start(staging[i % 4].rearrange("p (c o) -> p c o", c=CH),
                               weights[l, n].rearrange("(c p) o -> p c o", p=P)).then_inc(w_loaded[i % 4], 16)

            def load_bias(u):
                sync.wait_ge(neg_done, u.before(4).count(2 * HEADS, 2 * HEADS))
                sync.dma_start(bias[u.k % 4][:, :, :],
                               adj[bass.ds(u.graph(), 1)].rearrange("a (i p) k -> p (a i) k", p=P)
                               ).then_inc(bias_loaded[u.k % 4], 16)

            def load_rows(u):
                if u.own_rows:
                    if u.t > 2:
                        sync.wait_ge(stored[0], 16 * 2)
                else:
                    sync.wait_ge(result_done, u.before(4).count(TILES, TILES))
                sync.dma_start(rows_of(u)[:, :, :],
                               x[bass.ds(u.graph(), 1)].rearrange("a (i p) c -> p (a i) c", p=P)
                               ).then_inc(own_rows_loaded if u.own_rows else rows_loaded[u.t % 2], 16)

            def stack_quadrant(u, g):
                sync.wait_ge(scores_done, u.before(1).count(HEADS, CH * (g + 1)))
                quad = split_qk[g * HEAD:(g + 1) * HEAD, :, :].bitcast(F32)
                for part, (q, k) in enumerate(((1, 2), (1, 3), (0, 2))):
                    sync.dma_start(stack[part * HEAD:(part + 1) * HEAD, g, :, :].bitcast(F32),
                                   quad[:, q:k + 1:k - q, :]).then_inc(stacked[g], 16)

            first, second = Unit(0, None, UNITS), Unit(1, None, UNITS)
            load_rows(first)
            load_weights(0)
            load_weights(1)
            load_weights(2)
            load_bias(first)
            load_weights(3)
            for l in range(2):
                for tile, name in ((v_bias, "v"), (o_bias, "o")):
                    sync.dma_start(tile[l][:, :], biases[l, name].rearrange("(a c) -> a c", a=1).to_broadcast([P, H])
                                   ).then_inc(bias_rows_loaded, 16)
            load_bias(second)
            load_rows(second)
            for i in range(4, 8):
                sync.wait_ge(w_low_done, i - 3)
                load_weights(i)

            def slot(attend, project, output, norm):
                if norm is not None and norm.k > 1:
                    load_bias(norm)
                    if norm.layer == 0:
                        load_rows(norm)
                if project is not None:
                    sync.wait_ge(qk_low_done, project.count(CH, CH))
                    sync.sem_inc(passed, 1)
                    for g in range(QUADS - 1):
                        stack_quadrant(project, g)
                if output is not None and output.layer == 1:
                    sync.wait_ge(result_done, output.count(TILES, TILES))
                    sync.dma_start(out[bass.ds(output.graph(), 1)].rearrange("a (i p) c -> p (a i) c", p=P),
                                   rows_of(output)[:, :, :]).then_inc(stored[output.t % 2], 16)
                if project is not None:
                    stack_quadrant(project, QUADS - 1)

            program(slot, sync.Fori)
            for i in range(2):
                sync.wait_ge(stored[i], 16 * (B // 2))

        @block.gpsimd
        def _(pool):
            nc.gpsimd.memset(identity[:, :], 0.0).then_inc(constants_done, 1)
            nc.gpsimd.memset(minus_half[:, :], -0.5).then_inc(constants_done, 1)
            pool.wait_ge(constants_done, 2)
            nc.gpsimd.affine_select(out=identity[:, :], in_=identity[:, :], compare_op=ALU.not_equal, fill=1.0,
                                    base=0, pattern=[[-1, P]], channel_multiplier=1).then_inc(constants_done, 1)

            def invert_deviation(u, _=0):
                pool.wait_ge(mean_done, u.count(TILES, TILES))
                pool.sem_inc(passed, 1)
                nc.gpsimd.tensor_scalar(var_eps[:, :], mean_var[:, :, 1], EPS, None, ALU.add).then_inc(eps_done, 1)
                pool.wait_ge(eps_done, u.count(1, 1))
                nc.gpsimd.tensor_tensor(inv_dev[:, :], var_eps[:, :], minus_half[:, :], ALU.pow
                                        ).then_inc(inv_dev_done, 1)

            def add_half(u, step):
                pool.wait_ge(neg_done, u.count(2 * HEADS, 2 * step + 2))
                n = neg[:, step % NEG, :, :]
                nc.gpsimd.tensor_tensor(half[:, step % GROUP, :, :], n[:, :, 0:N // 2], n[:, :, N // 2:N], ALU.add
                                        ).then_inc(half_done, 1)

            def add_rest(u, g):
                pool.wait_ge(half_done, u.count(HEADS, GROUP * (g + 1)))
                nc.gpsimd.tensor_tensor(quarter[:, :, :, :], half[:, :, :, 0:N // 4], half[:, :, :, N // 4:N // 2],
                                        ALU.add).then_inc(quarter_done, 1)
                pool.wait_ge(quarter_done, u.count(GROUPS, g + 1))
                pool.wait_ge(guard_done, u.count(3 * GROUPS, 3 * g))
                nc.gpsimd.tensor_tensor(eighth[:, :, :, :], quarter[:, :, :, 0:N // 8], quarter[:, :, :, N // 8:N // 4],
                                        ALU.add).then_inc(eighth_done, 1)

            def split_heads(u, g):
                i = (u.k * GROUPS + g) % 2
                if g == 0:
                    pool.wait_ge(out_ready, u.before(1).count(TILES, TILES))
                pool.wait_ge(heads_done, u.count(GROUPS, g + 1))
                pool.sem_inc(passed, 1)
                nc.gpsimd.tensor_scalar(headsT_high[:, g, :], headsT[:, i, :], 1.0, 0.0, ALU.mult, ALU.add
                                        ).then_inc(heads_high_done, 1)
                pool.wait_ge(heads_high_done, u.count(GROUPS, g + 1))
                nc.gpsimd.tensor_tensor(headsT_low[:, g, :], headsT[:, i, :], headsT_high[:, g, :].bitcast(F32),
                                        ALU.subtract).then_inc(heads_split_done, 1)

            def add_output_bias(u, _):
                if u.k == 0:
                    pool.wait_ge(bias_rows_loaded, 16 * 4)
                pool.wait_ge(normed_done, u.count(TILES, TILES))
                r = rows_of(u)
                for i in range(TILES):
                    add = nc.gpsimd.tensor_tensor(r[:, i, :], r[:, i, :], o_bias[u.layer][:, :], ALU.add)
                add.then_inc(residual_done, 1)

            def split_value_and_output_weights():
                for i in range(6, 8):
                    l, name = matrices[i]
                    pool.wait_ge(w_high_done, i + 1)
                    nc.gpsimd.tensor_tensor(w_low[l, name][:, :, :].rearrange("p c o -> p (c o)"), staging[i % 4],
                                            w_high[l, name][:, :, :].rearrange("p c o -> p (c o)").bitcast(F32), ALU.subtract
                                            ).then_inc(vo_low_done, 1)

            invert_deviation(Unit(0, None, UNITS))

            def slot(attend, project, output, norm):
                for stage, u, i in (
                    (add_half, attend, 1), (add_half, attend, 2), (split_heads, output, 0), (add_half, attend, 3),
                    (add_rest, attend, 0), (split_heads, output, 1), (split_heads, output, 2),
                    (add_half, attend, 4), (add_half, attend, 5), (add_half, attend, 6), (add_half, attend, 7),
                    (add_rest, attend, 1), (add_half, attend, 8), (add_output_bias, project, 0),
                    (add_half, attend, 9), (invert_deviation, norm, 0), (add_half, attend, 10),
                    (add_half, attend, 11), (add_rest, attend, 2), (add_half, project, 0),
                ):
                    if u is not None and (stage != invert_deviation or u.k > 0):
                        stage(u, i)
                        if stage == invert_deviation and u.k == 1:
                            split_value_and_output_weights()

            program(slot, pool.Fori)

        @block.scalar
        def _(act):
            def weights_high(i):
                l, n = matrices[i]
                act.wait_ge(w_loaded[i % 4], 16 * (i // 4 + 1))
                scale = (SCALE / 2 if l == 0 else SCALE) if n == "q" else 1.0
                nc.scalar.activation(w_high[l, n][:, :, :].rearrange("p c o -> p (c o)"), staging[i % 4], ACT.Copy,
                                     scale=scale).then_inc(w_high_done, 1)

            def exps(u, step):
                act.wait_ge(probT_ready, u.count(HEADS, step + 1 - PROB))
                for q in range(TILES):
                    act.wait_ge(neg_done, u.count(2 * HEADS, 2 * step + q + 1))
                    nc.scalar.activation(prob[:, step % PROB, q, :], neg[:, step % NEG, q, :], ACT.Exp, scale=-1.0,
                                         bias=neg_max[u.k % 2][:, step, q:q + 1],
                                         accum_out=sums[u.k % 2][:, step, q:q + 1]).then_inc(exp_done, 1)

            def copy_probT(u, step):
                if u.k == 0 and step < PROBT:
                    act.wait_ge(vo_low_done, 2)
                act.wait_ge(probT_ready, u.count(HEADS, step + 1))
                act.wait_ge(heads_ready, u.count(GROUPS, (step - PROBT) // GROUP + 1))
                nc.scalar.activation(probT[:, step % PROBT, :, :].rearrange("p a b -> p (a b)"),
                                     probT_bank[step % 2][:, :], ACT.Copy).then_inc(act_copy_done, 1)

            def rows_high(u, i):
                act.wait_ge(rowsT_ready, u.count(TILES, i + 1))
                act.wait_ge(v_ready, u.before(1).count(TILES, 0))
                act.wait_ge(qk_ready, u.before(1).count(CH, 0))
                nc.scalar.activation(rowsT_high[u.k % 2][:, :, i * P:(i + 1) * P],
                                     misc_bank[MISC["rows"][i]][:, 0:H].rearrange("p (c t) -> p c t", c=CH), ACT.Relu
                                     ).then_inc(rows_high_done, 1)

            def qk_high(u, c):
                act.wait_ge(qk_ready, u.count(CH, c + 1))
                if c == 0:
                    for g in range(QUADS):
                        act.wait_ge(stacked[g], u.count(16 * COPIES, 0))
                nc.scalar.activation(split_qk[:, 1:3, c * N:(c + 1) * N],
                                     misc_bank[MISC["qk"][c]][:, :].rearrange("p (a n) -> p a n", a=2), ACT.Copy
                                     ).then_inc(qk_high_done, 1)

            def copy_sharesT(u, g):
                act.wait_ge(sharesT_ready, u.count(GROUPS, g + 1))
                act.wait_ge(heads_done, u.count(GROUPS, g))
                nc.scalar.activation(sharesT[:, :], values_bank[(u.k * GROUPS + g) % 2][:, N:2 * N], ACT.Copy
                                     ).then_inc(sharesT_done, 1)

            weights_high(0)
            weights_high(1)
            for i in range(TILES):
                rows_high(Unit(0, None, UNITS), i)
            weights_high(2)
            weights_high(3)

            def slot(attend, project, output, norm):
                for stage, u, i in (
                    (rows_high, project, 1), (exps, attend, 0), (copy_probT, output, 10),
                    (copy_sharesT, output, 1), (exps, attend, 1), (copy_probT, output, 11), (exps, attend, 2),
                    (exps, attend, 3), (copy_probT, attend, 0), (qk_high, project, 0), (exps, attend, 4),
                    (copy_sharesT, output, 2), (exps, attend, 5), (qk_high, project, 1), (exps, attend, 6),
                    (copy_probT, attend, 3), (qk_high, project, 2), (copy_probT, attend, 4), (exps, attend, 7),
                    (exps, attend, 8), (copy_probT, attend, 5), (copy_probT, attend, 6), (exps, attend, 9),
                    (copy_probT, attend, 7), (copy_probT, attend, 8), (exps, attend, 10), (exps, attend, 11),
                    (copy_sharesT, attend, 0), (copy_probT, attend, 9), (rows_high, norm, 0),
                ):
                    if u is not None and (stage != rows_high or u.k > 0):
                        stage(u, i)
                        if (stage, u.k, i) == (qk_high, 0, CH - 1):
                            for n in range(4, 8):
                                weights_high(n)

            program(slot, act.Fori)

        @block.vector
        def _(dve):
            def statistics(u, i):
                if u.layer == 1:
                    dve.wait_ge(result_done, u.layer_before().count(TILES, i + 1))
                elif u.own_rows:
                    dve.wait_ge(own_rows_loaded, 16 if u.t == 2 else 32)
                else:
                    dve.wait_ge(rows_loaded[u.t % 2], rows_count(u))
                nc.vector.bn_stats(stats[:, i, :], rows_of(u)[:, i, :]).then_inc(stats_done, 1)

            def rows_count(u):
                n = u.t // 2 + (u.t % 2 == 1 or u.t == 0)
                return 16 * n if u.turn is None else u.turn * 16 + 16 * n

            def bias_count(u):
                return 16 * (u.k // 4 + 1) if u.turn is None else u.turn * 16 + 16 * (u.k // 4 + 1)

            def mean(u, i):
                dve.wait_ge(stats_done, u.count(TILES, i + 1))
                dve.wait_ge(eps_done, u.count(1, 0))
                dve.sem_inc(passed, 1)
                nc.vector.bn_aggr(mean_var[:, i, :], stats[:, i, :]).then_inc(mean_done, 1)

            def normalise(u, i):
                dve.wait_ge(inv_dev_done, u.count(1, 1))
                dve.wait_ge(rowsT_ready, u.count(TILES, 0))
                nc.vector.tensor_scalar(normed[:, i, :], rows_of(u)[:, i, :], mean_var[:, i, 0:1], inv_dev[:, i:i + 1],
                                        ALU.subtract, ALU.mult).then_inc(normed_done, 1)

            def rows_low(u, i):
                dve.wait_ge(rows_high_done, u.count(TILES, i + 1))
                where = slice(i * P, (i + 1) * P)
                nc.vector.scalar_tensor_tensor(
                    out=rowsT_low[u.k % 2][:, :, where], in0=misc_bank[MISC["rows"][i]][:, 0:H].rearrange("p (c t) -> p c t", c=CH),
                    scalar=0.0, in1=rowsT_high[u.k % 2][:, :, where].bitcast(F32), op0=ALU.max, op1=ALU.subtract
                ).then_inc(rows_low_done, 1)

            def qk_low(u, c):
                dve.wait_ge(qk_high_done, u.count(CH, c + 1))
                where = slice(c * N, (c + 1) * N)
                nc.vector.tensor_tensor(split_qk[:, 0:4:3, where],
                                        misc_bank[MISC["qk"][c]][:, :].rearrange("p (a n) -> p a n", a=2),
                                        split_qk[:, 1:3, where].bitcast(F32), ALU.subtract).then_inc(qk_low_done, 1)

            def add_value_bias(u, i):
                dve.wait_ge(v_ready, u.count(TILES, i + 1))
                dve.wait_ge(heads_ready, u.before(1).count(GROUPS, 0))
                nc.vector.tensor_tensor(values[u.k % 2][:, i, :], misc_bank[MISC["v"][i]][:, 0:H], v_bias[u.layer][:, :],
                                        ALU.add).then_inc(values_done, 1)

            def negate_scores(u, step):
                if u.k == 0 and step == 0:
                    dve.wait_ge(w_low_done, 6)
                if step == 0:
                    dve.wait_ge(bias_loaded[u.k % 4], bias_count(u))
                dve.wait_ge(scores_done, u.count(HEADS, step + 1))
                dve.wait_ge(exp_done, u.count(2 * HEADS, 2 * (step + 1 - NEG)))
                dve.wait_ge(half_done, u.count(HEADS, step + 1 - NEG))
                dve.sem_inc(passed, 1)
                for q in range(TILES):
                    nc.vector.tensor_tensor_reduce(
                        out=neg[:, step % NEG, q, :], in0=score_bank[step % 2][:, q * N:(q + 1) * N],
                        in1=bias[u.k % 4][:, q, :], scale=-2.0 if u.layer == 0 else -1.0, scalar=LARGEST,
                        op0=ALU.add, op1=ALU.min, accum_out=neg_max[u.k % 2][:, step, q:q + 1]
                    ).then_inc(neg_done, 1)

            def copy_probT(u, step):
                if u.k == 0 and step < PROBT:
                    dve.wait_ge(vo_low_done, 2)
                dve.wait_ge(probT_ready, u.count(HEADS, step + 1))
                dve.wait_ge(heads_ready, u.count(GROUPS, (step - PROBT) // GROUP + 1))
                nc.vector.tensor_copy(probT[:, step % PROBT, :, :].rearrange("p a b -> p (a b)"),
                                      probT_bank[step % 2][:, :]).then_inc(dve_copy_done, 1)

            def share(u, g):
                heads = slice(GROUP * g, GROUP * (g + 1))
                i = (u.k * GROUPS + g) % 2
                dve.wait_ge(exp_done, u.count(2 * HEADS, 2 * GROUP * (g + 1)))
                nc.vector.reciprocal(inverse[i][:, :, :], sums[u.k % 2][:, heads, :].rearrange("p h q -> p q h")).then_inc(guard_done, 1)
                dve.wait_ge(eighth_done, u.count(GROUPS, g + 1))
                nc.vector.tensor_reduce(total[:, :, :].rearrange("p q h -> p h q"), eighth[:, :, :, :], AX.X, ALU.add).then_inc(guard_done, 1)
                dve.wait_ge(guard_done, u.count(3 * GROUPS, 3 * g + 2))
                nc.vector.scalar_tensor_tensor(out=nonzero[i][:, :, :], in0=total[:, :, :], scalar=-1.0,
                                               in1=neg_max[u.k % 2][:, heads, :].rearrange("p h q -> p q h"), op0=ALU.mult, op1=ALU.min
                                               ).then_inc(guard_done, 1)
                dve.wait_ge(guard_done, u.count(3 * GROUPS, 3 * g + 3))
                wide = [t[:, :, :].rearrange("p q (h a) -> p (q h) a", a=1).to_broadcast([P, TILES * GROUP, HEAD])
                        for t in (nonzero[i], inverse[i])]
                nc.vector.scalar_tensor_tensor(out=shares[:, i, :, :], in0=wide[0],
                                               scalar=0.0, in1=wide[1], op0=ALU.not_equal, op1=ALU.mult
                                               ).then_inc(shares_done, 1)

            def scale_heads(u, g):
                i = (u.k * GROUPS + g) % 2
                dve.wait_ge(heads_ready, u.count(GROUPS, g + 1))
                dve.wait_ge(sharesT_done, u.count(GROUPS, g + 1))
                dve.wait_ge(heads_split_done, u.count(GROUPS, g - 1))
                nc.vector.tensor_tensor(headsT[:, i, :], values_bank[i][:, 0:N], sharesT[:, :], ALU.mult
                                        ).then_inc(heads_done, 1)

            def result(u, i):
                dve.wait_ge(out_ready, u.count(TILES, i + 1))
                dve.wait_ge(residual_done, u.count(1, 1))
                to = own_rows if u.own_rows else rows[1][u.t % 2]
                if u.layer == 0 and i == 0 and not u.own_rows:
                    dve.wait_ge(stored[u.t % 2], stored_count(u))
                nc.vector.tensor_tensor(to[:, i, :], misc_bank[MISC["out"][i]][:, 0:H], rows_of(u)[:, i, :], ALU.add
                                        ).then_inc(result_done, 1)

            def stored_count(u):
                return 16 * (u.t // 2) if u.turn is None else u.turn * 16 + 16 * (u.t // 2)

            def weights_low(i):
                l, n = matrices[i]
                dve.wait_ge(w_high_done, i + 1)
                scale = (SCALE / 2 if l == 0 else SCALE) if n == "q" else 1.0
                nc.vector.scalar_tensor_tensor(
                    out=w_low[l, n][:, :, :].rearrange("p c o -> p (c o)"), in0=staging[i % 4], scalar=scale,
                    in1=w_high[l, n][:, :, :].rearrange("p c o -> p (c o)").bitcast(F32), op0=ALU.mult, op1=ALU.subtract
                ).then_inc(w_low_done, 1)

            first = Unit(0, None, UNITS)
            for i in range(TILES):
                statistics(first, i)
            for i in range(TILES):
                mean(first, i)
            for i in range(TILES):
                normalise(first, i)
            weights_low(0)
            weights_low(1)
            for i in range(TILES):
                rows_low(first, i)
            weights_low(2)
            weights_low(3)
            dve.wait_ge(bias_rows_loaded, 16 * 4)

            def slot(attend, project, output, norm):
                for stage, u, i in (
                    (negate_scores, attend, 0), (scale_heads, output, 0), (rows_low, project, 0),
                    (rows_low, project, 1), (negate_scores, attend, 1), (negate_scores, attend, 2),
                    (share, output, 2), (negate_scores, attend, 3), (scale_heads, output, 1),
                    (negate_scores, attend, 4), (copy_probT, attend, 1), (negate_scores, attend, 5),
                    (qk_low, project, 0), (scale_heads, output, 2), (copy_probT, attend, 2),
                    (negate_scores, attend, 6), (qk_low, project, 1), (negate_scores, attend, 7),
                    (negate_scores, attend, 8), (share, attend, 0), (result, output, 0), (statistics, norm, 0),
                    (qk_low, project, 2), (negate_scores, attend, 9), (share, attend, 1), (result, output, 1),
                    (statistics, norm, 1), (mean, norm, 0), (mean, norm, 1), (negate_scores, attend, 10),
                    (negate_scores, attend, 11), (add_value_bias, project, 0), (normalise, norm, 0),
                    (normalise, norm, 1), (add_value_bias, project, 1),
                ):
                    if u is not None and (stage not in (statistics, mean, normalise, rows_low) or u.k > 0):
                        stage(u, i)
                        if (stage, u.k, i) == (mean, 1, TILES - 1):
                            weights_low(4)
                            weights_low(5)

            program(slot, dve.Fori)

        @block.tensor
        def _(pe):
            def copied(u, steps):
                n = sum(s not in DVE_COPY_HEADS for s in range(steps))
                return n, steps - n

            def scores(u, step):
                g, c = step // CH, step % CH
                if c == 0:
                    pe.wait_ge(stacked[g], u.count(16 * COPIES, 16 * COPIES))
                pe.wait_ge(neg_done, u.count(2 * HEADS, 2 * (step - 1)))
                for q in range(TILES):
                    mm = nc.tensor.matmul(score_bank[step % 2][:, q * N:(q + 1) * N],
                                          stack[:, g, 0, c * N + q * P:c * N + (q + 1) * P],
                                          stack[:, g, 1, c * N:(c + 1) * N], start=True, stop=True)
                mm.then_inc(scores_done, 1)

            def transposes(u, step):
                pe.wait_ge(exp_done, u.count(2 * HEADS, 2 * (step + 1)))
                if step >= 2:
                    n = sum(s not in DVE_COPY_HEADS for s in range(step - 1))
                    pe.wait_ge(act_copy_done, u.count(ACT_COPIES, n))
                    pe.wait_ge(dve_copy_done, u.count(DVE_COPIES, step - 1 - n))
                else:
                    n = sum(s not in DVE_COPY_HEADS for s in range(HEADS + step - 1))
                    pe.wait_ge(act_copy_done, u.before(1).count(ACT_COPIES, n))
                    pe.wait_ge(dve_copy_done, u.before(1).count(DVE_COPIES, HEADS + step - 1 - n))
                for k in range(TILES):
                    for q in range(TILES):
                        mm = nc.tensor.transpose(probT_bank[step % 2][:, k * N + q * P:k * N + (q + 1) * P],
                                                 prob[:, step % PROB, q, k * P:(k + 1) * P], identity[:, :])
                mm.then_inc(probT_ready, 1)

            def weigh_values(u, g):
                i = (u.k * GROUPS + g) % 2
                n = sum(s not in DVE_COPY_HEADS for s in range(GROUP * (g + 1)))
                pe.wait_ge(act_copy_done, u.count(ACT_COPIES, n))
                pe.wait_ge(dve_copy_done, u.count(DVE_COPIES, GROUP * (g + 1) - n))
                if g == 0:
                    pe.wait_ge(values_done, u.count(TILES, TILES))
                pe.wait_ge(heads_done, u.count(GROUPS, g - 1))
                for k in range(TILES):
                    for a in range(GROUP):
                        h = GROUP * g + a
                        mm = nc.tensor.matmul(values_bank[i][a * HEAD:(a + 1) * HEAD, 0:N],
                                              values[u.k % 2][:, k, h * HEAD:(h + 1) * HEAD],
                                              probT[:, h % PROBT, k, :], start=(k == 0), stop=(k == TILES - 1))
                mm.then_inc(heads_ready, 1)

            def transpose_rows(u, i):
                pe.wait_ge(normed_done, u.count(TILES, i + 1))
                for c in range(CH):
                    mm = nc.tensor.transpose(misc_bank[MISC["rows"][i]][:, c * P:(c + 1) * P],
                                             normed[:, i, c * P:(c + 1) * P], identity[:, :])
                mm.then_inc(rowsT_ready, 1)

            def project_qk(u, c, which):
                if which == 0 and c == 0:
                    pe.wait_ge(rows_low_done, u.count(TILES, TILES))
                    if u.k == 0:
                        pe.wait_ge(w_low_done, 2)
                    if u.k == 3:
                        pe.wait_ge(w_low_done, 6)
                        pe.wait_ge(vo_low_done, 2)
                high, low = w_high[u.layer, "qk"[which]], w_low[u.layer, "qk"[which]]
                r_high, r_low = rowsT_high[u.k % 2], rowsT_low[u.k % 2]
                cols = slice(c * P, (c + 1) * P)
                into = misc_bank[MISC["qk"][c]][:, which * N:(which + 1) * N]
                for k in range(CH):
                    for n, (w, r) in enumerate(((low, r_high), (high, r_low), (high, r_high))):
                        mm = nc.tensor.matmul(into, w[:, k, cols], r[:, k, :], start=(k == 0 and n == 0),
                                              stop=(k == CH - 1 and n == 2))
                if which == 1:
                    mm.then_inc(qk_ready, 1)

            def project_queries(u, c):
                project_qk(u, c, 0)

            def project_keys(u, c):
                project_qk(u, c, 1)

            def project_v(u, i):
                if u.k == 0:
                    pe.wait_ge(w_low_done, 3)
                high, low = w_high[u.layer, "v"], w_low[u.layer, "v"]
                r_high, r_low = rowsT_high[u.k % 2], rowsT_low[u.k % 2]
                where = slice(i * P, (i + 1) * P)
                for k in range(CH):
                    for n, (r, w) in enumerate(((r_low, high), (r_high, low), (r_high, high))):
                        mm = nc.tensor.matmul(misc_bank[MISC["v"][i]][:, 0:H], r[:, k, where], w[:, k, :],
                                              start=(k == 0 and n == 0), stop=(k == CH - 1 and n == 2))
                mm.then_inc(v_ready, 1)

            def transpose_shares(u, g):
                pe.wait_ge(shares_done, u.count(GROUPS, g + 1))
                s = shares[:, (u.k * GROUPS + g) % 2, :, :].rearrange("p a b -> p (a b)")
                for q in range(TILES):
                    mm = nc.tensor.transpose(values_bank[(u.k * GROUPS + g) % 2][:, N + q * P:N + (q + 1) * P],
                                             s[:, q * P:(q + 1) * P], identity[:, :])
                mm.then_inc(sharesT_ready, 1)

            def project_out(u, i):
                pe.wait_ge(heads_split_done, u.count(GROUPS, GROUPS))
                if u.k == 0:
                    pe.wait_ge(w_low_done, 4)
                high, low = w_high[u.layer, "o"], w_low[u.layer, "o"]
                where = slice(i * P, (i + 1) * P)
                for k in range(CH):
                    for n, (r, w) in enumerate(((headsT_low, high), (headsT_high, low), (headsT_high, high))):
                        mm = nc.tensor.matmul(misc_bank[MISC["out"][i]][:, 0:H], r[:, k, where], w[:, k, :],
                                              start=(k == 0 and n == 0), stop=(k == CH - 1 and n == 2))
                mm.then_inc(out_ready, 1)

            uses = {transpose_rows: ("rows", rows_low_done, TILES), project_queries: ("qk", qk_low_done, CH),
                    project_v: ("v", values_done, TILES), project_out: ("out", result_done, TILES)}
            last_use = [None, None]

            def use_bank(stage, u, i, wait=True):
                bank = MISC[uses[stage][0]][i]
                if wait and last_use[bank] is not None:
                    before, v, n = last_use[bank]
                    _, read, per_unit = uses[before]
                    pe.wait_ge(read, v.count(per_unit, n + 1))
                last_use[bank] = (stage, u, i)

            def stages(attend, project, output, norm):
                return (
                    (weigh_values, output, 1), (transpose_shares, output, 1), (scores, attend, 1),
                    (transposes, output, 11), (scores, attend, 2), (project_queries, project, 0),
                    (scores, attend, 3), (transposes, attend, 0), (project_keys, project, 0),
                    (weigh_values, output, 2), (scores, attend, 4), (transposes, attend, 1), (scores, attend, 5),
                    (transpose_shares, output, 2), (project_queries, project, 1), (transposes, attend, 2),
                    (project_keys, project, 1), (scores, attend, 6), (transposes, attend, 3), (scores, attend, 7),
                    (project_queries, project, 2), (transposes, attend, 4), (scores, attend, 8),
                    (project_keys, project, 2), (project_out, output, 0), (scores, attend, 9),
                    (transposes, attend, 5), (transposes, attend, 6), (weigh_values, attend, 0),
                    (project_out, output, 1), (transposes, attend, 7), (transposes, attend, 8),
                    (scores, attend, 10), (scores, attend, 11), (project_v, project, 0), (project_v, project, 1),
                    (transpose_shares, attend, 0), (transposes, attend, 9), (transposes, attend, 10),
                    (scores, project, 0), (transpose_rows, norm, 0), (transpose_rows, norm, 1),
                )

            def slot(attend, project, output, norm):
                if attend is not None and attend.turn is not None and attend.k == LOOPED:
                    for stage, u, i in stages(attend.before(1), attend, output.before(1), project):
                        if stage in uses:
                            use_bank(stage, u, i, wait=False)
                for stage, u, i in stages(attend, project, output, norm):
                    if u is not None:
                        if stage in uses:
                            use_bank(stage, u, i)
                        stage(u, i)

            program(slot, pe.Fori)


def kernel(x, adj, L0_gnn_Wq, L0_gnn_Wk, L0_gnn_Wv, L0_gnn_bv, L0_gnn_Wo, L0_gnn_bo,
           L1_gnn_Wq, L1_gnn_Wk, L1_gnn_Wv, L1_gnn_bv, L1_gnn_Wo, L1_gnn_bo):
    import numpy as np
    import concourse.bacc as bacc
    from concourse.bass_utils import run_bass_kernel_spmd

    nc = bacc.Bacc("TRN2", target_bir_lowering=False, num_devices=1)
    arrays = {"x": np.ascontiguousarray(x), "adj": np.ascontiguousarray(adj)}
    for l, ws in enumerate(((L0_gnn_Wq, L0_gnn_Wk, L0_gnn_Wv, L0_gnn_Wo), (L1_gnn_Wq, L1_gnn_Wk, L1_gnn_Wv, L1_gnn_Wo))):
        for n, w in zip("qkvo", ws):
            w = np.asarray(w).T
            if n in "qk":
                w = w.reshape(w.shape[0], 4, 3, 32).transpose(0, 2, 1, 3).reshape(w.shape)
            arrays[f"w{l}{n}"] = np.ascontiguousarray(w)
    for l, bs in enumerate(((L0_gnn_bv, L0_gnn_bo), (L1_gnn_bv, L1_gnn_bo))):
        for n, b in zip("vo", bs):
            arrays[f"b{l}{n}"] = np.ascontiguousarray(b)
    ins = {n: nc.dram_tensor(n, a.shape, F32, kind="ExternalInput").ap() for n, a in arrays.items()}
    out = nc.dram_tensor("out", arrays["x"].shape, F32, kind="ExternalOutput").ap()
    build(nc, ins["x"], ins["adj"], {(l, n): ins[f"w{l}{n}"] for l in range(2) for n in "qkvo"},
          {(l, n): ins[f"b{l}{n}"] for l in range(2) for n in "vo"}, out)
    r = run_bass_kernel_spmd(nc, [arrays], core_ids=[0])
    return r.results[0]["out"]
```
